# Optimizing a Trainium2 kernel written in Bass

```python
import numpy as np
import jax
import jax.numpy as jnp

def _softmax(x, axis=-1):
    return jax.nn.softmax(x, axis=axis)

def _gelu(x):
    return jax.nn.gelu(x, approximate=True)

def _silu(x):
    return jax.nn.silu(x)

def _sigmoid(x):
    return jax.nn.sigmoid(x)

def _layernorm(x, axis=-1, eps=1e-05):
    m = jnp.mean(x, axis=axis, keepdims=True)
    v = jnp.var(x, axis=axis, keepdims=True)
    return (x - m) / jnp.sqrt(v + eps)

def _scatter_add(tgt, idx, src, axis=0):
    return tgt.at[idx].add(src)

def _segment_sum(src, seg, n):
    return jax.ops.segment_sum(src, seg, n)
kernel_name = 'mk_xattn_ffn_d1_seqx_r8_3459d7'

def setup_inputs(seed: int=0):
    np.random.seed(seed)
    _w = jnp.asarray

    def _rec_inputs():
        import jax
        import jax.numpy as jnp
        _rk = jax.random.key(seed)
        x = -0.0002928 + 1 * jax.random.normal(jax.random.fold_in(_rk, 1), (4, 256, 256), jnp.float32)
        _lenS = 256 - jax.random.randint(jax.random.fold_in(_rk, 7), (4,), 0, max(1, 256 // 4) + 1, jnp.int32)
        _lenS2 = 64 - jax.random.randint(jax.random.fold_in(_rk, 8), (4,), 0, max(1, 64 // 4) + 1, jnp.int32)
        _ctx_512P = jax.random.normal(jax.random.fold_in(_rk, 11), (4, 16, 64), jnp.float32)
        _ctx_512c = jax.random.dirichlet(jax.random.fold_in(_rk, 511), 0.3 * jnp.ones((16,), jnp.float32), (4, 64))
        _ctx_512t = jnp.einsum('bsk,bkd->bsd', _ctx_512c, _ctx_512P)
        _ctx_512t = _ctx_512t * jax.lax.rsqrt(jnp.mean(jnp.square(_ctx_512t)) + 1e-12) * 0.953939
        ctx_512 = 0.000227908 + 0.99994 * (_ctx_512t + 0.3 * jax.random.normal(jax.random.fold_in(_rk, 611), (4, 64, 64), jnp.float32))
        return (x, ctx_512)
    x, ctx_512 = _rec_inputs()

    def _L0_xattn_setup():
        import jax, jax.numpy as jnp
        import numpy as np
        B, S, L = (2, 128, 128)
        DIM_Q, H, K, D_C, D_CQ, R = (256, 16, 128, 64, 192, 64)

        def _rope_tables(seq_len, dim, dtype):
            inv_freq = 1.0 / 10000.0 ** (jnp.arange(0, dim, 2, dtype=dtype) / dim)
            t = jnp.arange(seq_len, dtype=dtype)
            freqs = t[:, None] * inv_freq[None, :]
            sin = jnp.repeat(jnp.sin(freqs), 2, axis=-1)
            cos = jnp.repeat(jnp.cos(freqs), 2, axis=-1)
            return (sin, cos)

        def _rotate_half(x):
            h = x.shape[-1] // 2
            return jnp.concatenate([-x[..., h:], x[..., :h]], axis=-1)
        key = jax.random.key(seed)
        ks = jax.random.split(key, 8)
        s_in = 1.0 / np.sqrt(DIM_Q)
        s_k = 1.0 / np.sqrt(K)
        s_cq = 1.0 / np.sqrt(D_CQ)
        s_c = 1.0 / np.sqrt(D_C)
        return {'hidden_q': jax.random.normal(ks[0], (B, S, DIM_Q), jnp.float32), 'kv_c': jax.random.normal(ks[1], (B, L, D_C), jnp.float32), 'Wq': jax.random.normal(ks[2], (H * K, DIM_Q), jnp.float32) * s_in, 'w_kc_q': jax.random.normal(ks[3], (H, K, D_CQ), jnp.float32) * s_k, 'w_kc_kv': jax.random.normal(ks[4], (H, K, D_C), jnp.float32) * s_k, 'W_qr': jax.random.normal(ks[5], (H, D_CQ, R), jnp.float32) * s_cq / np.sqrt(R), 'W_kr': jax.random.normal(ks[6], (H, D_C, R), jnp.float32) * s_c, 'Wo': jax.random.normal(ks[7], (DIM_Q, H * K), jnp.float32) * s_k}
    _L0_xattn_all = _L0_xattn_setup()
    _L0_xattn_in = {k: v for k, v in _L0_xattn_all.items() if k in ('Wq', 'w_kc_q', 'w_kc_kv', 'W_qr', 'W_kr', 'Wo')}
    del _L0_xattn_all

    def _L0_ffn_setup():
        import jax, jax.numpy as jnp
        import numpy as np
        from jax import lax
        E = 64
        H = 256
        I = 88
        G = 8
        TOPK_GROUP = 4
        K = 8
        B, S = (2, 256)
        N = B * S
        CAP = 2 * N * K // E
        SCALE = 2.5

        def _route(x, router_weight, e_bias):
            logits = x.astype(jnp.float32) @ router_weight.astype(jnp.float32).T
            scores = jax.nn.sigmoid(logits)
            sc = scores + e_bias
            n = x.shape[0]
            group_scores = lax.top_k(sc.reshape(n, G, E // G), 2)[0].sum(-1)
            grp_idx = lax.top_k(group_scores, TOPK_GROUP)[1]
            group_mask = jnp.zeros((n, G), jnp.float32).at[jnp.arange(n)[:, None], grp_idx].set(1.0)
            score_mask = jnp.repeat(group_mask, E // G, axis=1)
            masked = jnp.where(score_mask > 0, sc, 0.0)
            topk_idx = lax.top_k(masked, K)[1]
            topk_w = jnp.take_along_axis(scores, topk_idx, axis=1)
            topk_w = topk_w / (topk_w.sum(-1, keepdims=True) + 1e-20)
            return (topk_idx, topk_w * SCALE)

        def _moe_experts(x, topk_idx, topk_w, w_gate, w_up, w_down):
            n = x.shape[0]
            flat_e = topk_idx.reshape(-1)
            rows = jnp.repeat(jnp.arange(n), K)
            oh = jax.nn.one_hot(flat_e, E, dtype=jnp.int32)
            pos = jnp.cumsum(oh, axis=0) - oh
            pos = jnp.take_along_axis(pos, flat_e[:, None], axis=1)[:, 0]
            valid = (pos < CAP).astype(x.dtype)
            p = jnp.minimum(pos, CAP - 1)
            buf = jnp.zeros((E, CAP, H), x.dtype).at[flat_e, p].add(x[rows] * valid[:, None])
            g = jnp.einsum('ech,ehi->eci', buf, w_gate)
            u = jnp.einsum('ech,ehi->eci', buf, w_up)
            y = jnp.einsum('eci,eih->ech', jax.nn.silu(g) * u, w_down)
            y_tok = y[flat_e, p] * (topk_w.reshape(-1) * valid)[:, None]
            return jnp.zeros((n, H), x.dtype).at[rows].add(y_tok)

        def _shared_mlp(x, sh_gate, sh_up, sh_down):
            return jax.nn.silu(x @ sh_gate) * (x @ sh_up) @ sh_down
        key = jax.random.key(seed)
        ks = jax.random.split(key, 9)
        f32 = jnp.float32
        return {'hidden_states': jax.random.normal(ks[0], (B, S, H), f32), 'router_weight': jax.random.normal(ks[1], (E, H), f32) * (2.0 / H) ** 0.5, 'e_bias': jnp.zeros((E,), f32), 'w_gate': jax.random.normal(ks[2], (E, H, I), f32) * (1.0 / H) ** 0.5, 'w_up': jax.random.normal(ks[3], (E, H, I), f32) * (1.0 / H) ** 0.5, 'w_down': jax.random.normal(ks[4], (E, I, H), f32) * (1.0 / I) ** 0.5, 'sh_gate': jax.random.normal(ks[5], (H, I), f32) * (1.0 / H) ** 0.5, 'sh_up': jax.random.normal(ks[6], (H, I), f32) * (1.0 / H) ** 0.5, 'sh_down': jax.random.normal(ks[7], (I, H), f32) * (1.0 / I) ** 0.5}
    _L0_ffn_all = _L0_ffn_setup()
    _L0_ffn_in = {k: v for k, v in _L0_ffn_all.items() if k in ('router_weight', 'e_bias', 'w_gate', 'w_up', 'w_down', 'sh_gate', 'sh_up', 'sh_down')}
    del _L0_ffn_all
    return {'x': x, 'ctx_512': ctx_512, 'L0_xattn_Wq': _L0_xattn_in['Wq'], 'L0_xattn_w_kc_q': _L0_xattn_in['w_kc_q'], 'L0_xattn_w_kc_kv': _L0_xattn_in['w_kc_kv'], 'L0_xattn_W_qr': _L0_xattn_in['W_qr'], 'L0_xattn_W_kr': _L0_xattn_in['W_kr'], 'L0_xattn_Wo': _L0_xattn_in['Wo'], 'L0_ffn_router_weight': _L0_ffn_in['router_weight'], 'L0_ffn_e_bias': _L0_ffn_in['e_bias'], 'L0_ffn_w_gate': _L0_ffn_in['w_gate'], 'L0_ffn_w_up': _L0_ffn_in['w_up'], 'L0_ffn_w_down': _L0_ffn_in['w_down'], 'L0_ffn_sh_gate': _L0_ffn_in['sh_gate'], 'L0_ffn_sh_up': _L0_ffn_in['sh_up'], 'L0_ffn_sh_down': _L0_ffn_in['sh_down']}

def reference(x, ctx_512, L0_xattn_Wq, L0_xattn_w_kc_q, L0_xattn_w_kc_kv, L0_xattn_W_qr, L0_xattn_W_kr, L0_xattn_Wo, L0_ffn_router_weight, L0_ffn_e_bias, L0_ffn_w_gate, L0_ffn_w_up, L0_ffn_w_down, L0_ffn_sh_gate, L0_ffn_sh_up, L0_ffn_sh_down):
    import jax
    import jax.numpy as jnp

    def _L0_xattn_ref(hidden_q, kv_c, Wq, w_kc_q, w_kc_kv, W_qr, W_kr, Wo):
        import jax, jax.numpy as jnp
        import numpy as np
        B, S, L = (2, 128, 128)
        DIM_Q, H, K, D_C, D_CQ, R = (256, 16, 128, 64, 192, 64)

        def _rope_tables(seq_len, dim, dtype):
            inv_freq = 1.0 / 10000.0 ** (jnp.arange(0, dim, 2, dtype=dtype) / dim)
            t = jnp.arange(seq_len, dtype=dtype)
            freqs = t[:, None] * inv_freq[None, :]
            sin = jnp.repeat(jnp.sin(freqs), 2, axis=-1)
            cos = jnp.repeat(jnp.cos(freqs), 2, axis=-1)
            return (sin, cos)

        def _rotate_half(x):
            h = x.shape[-1] // 2
            return jnp.concatenate([-x[..., h:], x[..., :h]], axis=-1)
        b, s, _ = hidden_q.shape
        l = kv_c.shape[1]
        q_hk = (hidden_q @ Wq.T).reshape(b, s, H, K)
        q_big = jnp.einsum('bshk,hkq->bshq', q_hk, w_kc_q)
        sin, cos = _rope_tables(l, D_C, kv_c.dtype)
        kv_rope = kv_c * cos[None] + _rotate_half(kv_c) * sin[None]
        q_r = jnp.einsum('bshq,hqr->bhsr', q_big, W_qr)
        k_r = jnp.einsum('bld,hdr->bhlr', kv_rope, W_kr)
        scores = jnp.einsum('bhsr,bhlr->bhsl', q_r, k_r)
        attn = jax.nn.softmax(scores, axis=-1)
        ctx_c = jnp.einsum('bhsl,bld->bhsd', attn, kv_rope)
        ctx_lat = jnp.einsum('bhsd,hkd->bshk', ctx_c, w_kc_kv)
        out = ctx_lat.reshape(b, s, H * K) @ Wo.T
        return out

    def _L0_ffn_ref(hidden_states, router_weight, e_bias, w_gate, w_up, w_down, sh_gate, sh_up, sh_down):
        import jax, jax.numpy as jnp
        import numpy as np
        from jax import lax
        E = 64
        H = 256
        I = 88
        G = 8
        TOPK_GROUP = 4
        K = 8
        B, S = (2, 256)
        N = B * S
        CAP = 2 * N * K // E
        SCALE = 2.5

        def _route(x, router_weight, e_bias):
            logits = x.astype(jnp.float32) @ router_weight.astype(jnp.float32).T
            scores = jax.nn.sigmoid(logits)
            sc = scores + e_bias
            n = x.shape[0]
            group_scores = lax.top_k(sc.reshape(n, G, E // G), 2)[0].sum(-1)
            grp_idx = lax.top_k(group_scores, TOPK_GROUP)[1]
            group_mask = jnp.zeros((n, G), jnp.float32).at[jnp.arange(n)[:, None], grp_idx].set(1.0)
            score_mask = jnp.repeat(group_mask, E // G, axis=1)
            masked = jnp.where(score_mask > 0, sc, 0.0)
            topk_idx = lax.top_k(masked, K)[1]
            topk_w = jnp.take_along_axis(scores, topk_idx, axis=1)
            topk_w = topk_w / (topk_w.sum(-1, keepdims=True) + 1e-20)
            return (topk_idx, topk_w * SCALE)

        def _moe_experts(x, topk_idx, topk_w, w_gate, w_up, w_down):
            n = x.shape[0]
            flat_e = topk_idx.reshape(-1)
            rows = jnp.repeat(jnp.arange(n), K)
            oh = jax.nn.one_hot(flat_e, E, dtype=jnp.int32)
            pos = jnp.cumsum(oh, axis=0) - oh
            pos = jnp.take_along_axis(pos, flat_e[:, None], axis=1)[:, 0]
            valid = (pos < CAP).astype(x.dtype)
            p = jnp.minimum(pos, CAP - 1)
            buf = jnp.zeros((E, CAP, H), x.dtype).at[flat_e, p].add(x[rows] * valid[:, None])
            g = jnp.einsum('ech,ehi->eci', buf, w_gate)
            u = jnp.einsum('ech,ehi->eci', buf, w_up)
            y = jnp.einsum('eci,eih->ech', jax.nn.silu(g) * u, w_down)
            y_tok = y[flat_e, p] * (topk_w.reshape(-1) * valid)[:, None]
            return jnp.zeros((n, H), x.dtype).at[rows].add(y_tok)

        def _shared_mlp(x, sh_gate, sh_up, sh_down):
            return jax.nn.silu(x @ sh_gate) * (x @ sh_up) @ sh_down
        orig_shape = hidden_states.shape
        x = hidden_states.reshape(-1, H)
        topk_idx, topk_w = _route(x, router_weight, e_bias)
        moe_out = _moe_experts(x, topk_idx, topk_w.astype(x.dtype), w_gate, w_up, w_down)
        out = moe_out + _shared_mlp(x, sh_gate, sh_up, sh_down)
        return out.reshape(orig_shape)
    x = x + _L0_xattn_ref(_layernorm(x, axis=-1), ctx_512, L0_xattn_Wq, L0_xattn_w_kc_q, L0_xattn_w_kc_kv, L0_xattn_W_qr, L0_xattn_W_kr, L0_xattn_Wo)
    x = x + _L0_ffn_ref(_layernorm(x, axis=-1), L0_ffn_router_weight, L0_ffn_e_bias, L0_ffn_w_gate, L0_ffn_w_up, L0_ffn_w_down, L0_ffn_sh_gate, L0_ffn_sh_up, L0_ffn_sh_down)
    return x

_drawn_inputs = setup_inputs


def setup_inputs(seed=0):
    import zlib

    import numpy as np

    out = dict(_drawn_inputs(seed))
    spreads = {'L0_ffn_e_bias': (0.0, 0.1)}
    factors = {}
    for name, (base, spread) in spreads.items():
        noise = np.random.default_rng([zlib.crc32(name.encode()), seed]).standard_normal(out[name].shape)
        drawn = base * np.exp(spread * noise) if base else spread * noise
        out[name] = jnp.asarray(drawn.astype(out[name].dtype))
    for name, factor in factors.items():
        out[name] = (out[name] * factor).astype(out[name].dtype)
    return out
```

```python
import concourse.bass as bass
from concourse import mybir
from contextlib import ExitStack

P = 128
BATCH, SEQ, DIM = 4, 256, 256
TOK = BATCH * SEQ
TILES = TOK // P
TPB = SEQ // P
KEYS, DC = 64, 64
HEADS, HK, DQ, RK = 16, 128, 192, 64
PAIRS = HEADS // 2
QC = 2
QP = DQ // QC
CH = DIM // P
EXP, GRP, EPG = 64, 8, 8
TOPG, TOPK, FF = 4, 8, 88
CAP = 128
SLOT_HI, SLOT_LO = 8, 16
SCALE = 2.5
EPS = 1e-5
RT = 2
CHUNKS = TILES // RT
BIG = 3.0e38
UNPICKED = 2048.0
FAR = CAP - UNPICKED

C_IDENT = 0
C_DIAG = C_IDENT + P
C_KEY = C_DIAG + EPG * EPG
C_HI = C_KEY + EXP
C_LO = C_HI + SLOT_HI
C_TOK = C_LO + SLOT_LO
C_COS = C_TOK + TILES
C_SIN = C_COS + DC
C_TRI = C_SIN + DC
C_ALL = C_TRI + P


def program(nc, a, out, dbg):
    f32, f16, i32, u32 = mybir.dt.float32, mybir.dt.float16, mybir.dt.int32, mybir.dt.uint32
    ALU, ACT, AX = mybir.AluOpType, mybir.ActivationFunctionType, mybir.AxisListType
    ctx = ExitStack()
    with ctx:
        def sb(name, shape, dt=f32):
            return ctx.enter_context(nc.sbuf_tensor(name, shape, dt))

        def sem(name):
            return ctx.enter_context(nc.semaphore(name))

        xn_table = nc.dram_tensor("xn_table", (TOK, DIM), f32, kind="Internal").ap()
        y_table = nc.dram_tensor("y_table", (EXP * CAP, DIM), f32, kind="Internal").ap()

        const = sb("const", [P, C_ALL])
        x = sb("x", [P, TILES, DIM])
        hn = sb("hn", [P, TILES, DIM])
        hnT = sb("hnT", [P, CH, TOK])
        bd = sb("bd", [P, BATCH, 2, KEYS])
        g_sb = sb("g_sb", [P, CH, BATCH, PAIRS, P])
        v_sb = sb("v_sb", [P, BATCH, PAIRS, DIM])
        region = sb("region", [P, 26624])
        small = sb("small", [P, 2048])
        tri16 = sb("tri16", [P, P], f16)
        ones16 = sb("ones16", [P, P], f16)

        def view(base, off, *dims):
            n = 1
            for d in dims:
                n *= d
            ap = base[:, off:off + n]
            if len(dims) == 2:
                ap = ap.rearrange("p (a b) -> p a b", b=dims[1])
            if len(dims) == 3:
                ap = ap.rearrange("p (a b c) -> p a b c", b=dims[1], c=dims[2])
            if len(dims) == 4:
                ap = ap.rearrange("p (a b c d) -> p a b c d", b=dims[1], c=dims[2], d=dims[3])
            return ap

        wkcq = view(region, 0, HEADS, QC, HK)
        wqr = view(region, 4096, HEADS, DQ)
        wkr = view(region, 7168, HEADS, DC)
        d_sb = view(region, 8192, HEADS, QC, DC)
        e_sb = view(region, 10240, HEADS, DC)
        wkv = view(region, 11264, HEADS, DC)
        wq = view(region, 12288, HEADS, DIM)
        wo = view(region, 16384, HEADS, DIM)
        c_sb = view(region, 20480, PAIRS, DIM)
        f_sb = view(region, 22528, PAIRS, DIM)
        ctx_sb = view(region, 24576, 2, DC)
        kvr = view(region, 24704, 2, 2 * DC)
        kvt = view(region, 24960, 2, DC)
        sc_sb = view(region, 0, 2, HEADS * KEYS)
        p_sb = view(region, 2048, 2, HEADS * KEYS)
        pt_sb = view(region, 4096, 2, PAIRS, P)
        hi_oh = region[:, 6144:6144 + 2048].bitcast(f16).rearrange(
            "p (t e a) -> p t e a", t=TILES, a=SLOT_HI)
        lo_oh = region[:, 8192:8192 + 4096].bitcast(f16).rearrange(
            "p (t e b) -> p t e b", t=TILES, b=SLOT_LO)
        WG = EPG * 2 * CH * FF
        WD = EPG * DIM
        WSLOTS = 3
        wgu_sb = [view(region, 12288 + s * (WG + WD), EPG, 2 * CH, FF) for s in range(WSLOTS - 1)]
        wdn_sb = [view(region, 12288 + s * (WG + WD) + WG, EPG, DIM) for s in range(WSLOTS - 1)]
        wgu_sb.append(view(region, 0, EPG, 2 * CH, FF))
        wdn_sb.append(view(region, WG, EPG, DIM))
        g_flat = g_sb[:, :, :, :, :].rearrange("p a b c d -> p (a b c d)")
        v_flat = v_sb[:, :, :, :].rearrange("p a b c -> p (a b c)")
        xg = [view(g_flat, s * 2048, EPG, DIM) for s in range(2)]
        xt = [view(g_flat, 4096 + s * 2048, CH, GRP, CAP) for s in range(2)]
        sg = [view(v_flat, s * 256, 2, CAP) for s in range(2)]
        ht = [view(v_flat, 512 + s * 256, 2, CAP) for s in range(2)]
        YS = 4
        ysb = [view(v_flat, 1024 + s * 512, 2, DIM) for s in range(YS)]
        RING = 16
        yg = [view(v_flat, 3072 + s * 256, DIM) for s in range(RING)]
        sg_sh = view(v_flat, 7168, 512)
        h_sh = view(region, 22016, TOK)

        at = [0]

        def take(*dims):
            n = 1
            for d in dims:
                n *= d
            v = view(small, at[0], *dims)
            at[0] += n
            return v
        rmax, rsum = take(2, HEADS), take(2, HEADS)
        stats, mv = take(TILES, 6), take(TILES, 2)
        veps, rs0, rs1, rstd = take(TILES), take(TILES), take(TILES), take(TILES)
        neghalf = take(1)
        ebias = take(EXP)
        el, s0, sc = take(RT, EXP), take(RT, EXP), take(RT, EXP)
        m1, n1 = take(RT, GRP, 4), take(RT, GRP, 4)
        m2, n2, t2 = take(RT, GRP, 2), take(RT, GRP, 2), take(RT, GRP, 2)
        gs, n3, t3 = take(RT, GRP), take(RT, GRP), take(RT, GRP)
        top4 = take(RT, 8)
        gpad = take(RT, 16)
        gpick = take(RT, GRP)
        msk, rep = take(RT, EXP), take(RT, EXP)
        top8 = take(RT, 8)
        key8 = take(TILES, TOPK)
        wgt8 = take(TILES, TOPK)
        wsum, wrec = take(TILES), take(TILES)
        key1 = take(RT, EXP)
        shw = sb("shw", [P, 2 * CH, FF])
        shd = view(region, 24064, DIM)
        rw = sb("rw", [P, CH, EXP])
        pick16 = region[:, 24320:24576].bitcast(f16).rearrange("p (t e) -> p t e", e=EXP)
        base16 = sb("base16", [P, CHUNKS + 1, EXP], f16)
        wsel = view(region, 25216, TILES, EXP)
        keys = view(region, 25728, TILES, EXP)
        slot_i = region[:, 26240:26368].bitcast(i32).rearrange("p (r e) -> p r e", e=EXP)
        hi_i = region[:, 26368:26496].bitcast(i32).rearrange("p (r e) -> p r e", e=EXP)
        lo_i = region[:, 26496:26624].bitcast(i32).rearrange("p (r e) -> p r e", e=EXP)
        idx_p = view(v_flat, 7680, P)
        idx_t = sb("idx_t", [P, EXP], u32)
        rows8 = sb("rows8", [P, TILES * TOPK], u32)
        idx_d = hnT[0:EXP, 0, :].rearrange("p (g i b) -> p g i b", g=GRP, b=SLOT_LO)
        eq = view(region, 23040, TOPK, EXP)
        eqw = view(region, 23552, TOPK, EXP)
        ident = const[:, C_IDENT:C_IDENT + P]

        bank = [ctx.enter_context(nc.psum_tensor(f"bank{i}", [P, 512], f32)) for i in range(8)]

        names = ("ld_const ld_x ld_ctx ld_wqr ld_wkcq ld_wq ld_wkv ld_wo ld_router ld_sh "
                 "ctx_roped bd_zero prep_mm prep_act prep_dve stats1 rstd1 hn1 "
                 "scores sc_free expd rsum_ok probs pt pt_sb attn x_ok stats2 rstd2 hn2 xn_wr "
                 "hn2T hn2T_sb logits elog pick base slotnum slot_read onehot keyed "
                 "sh_gu sh_act sh_h sh_dn sh_added idx_mm idx_dve idx_tr idx_ok "
                 "tr xt_ok gu silu h dn y_ok "
                 "rows wgt added outd d_chain a_chain p_chain small_ok").split()
        S = {n: sem(n) for n in names}
        s_w = [sem(f"ld_expert{s}") for s in range(WSLOTS)]
        s_xg = [sem(f"gathered{s}") for s in range(2)]
        s_yw = [sem(f"y_written{s}") for s in range(YS)]
        s_yg = [sem(f"y_gathered{s}") for s in range(RING)]

        block = ctx.enter_context(nc.Block())

        items = ([("K", 0)] + [("D", n) for n in range(4)] + [("E", n) for n in range(2)]
                 + [("C", n) for n in range(4)] + [("F", n) for n in range(4)]
                 + [("H", n) for n in range(4)] + [("G", n) for n in range(16)]
                 + [("V", n) for n in range(16)])
        NI = len(items)

        def out_by(n):
            return n // 2 + 1, (n + 1) // 2

        def last_of(kind):
            return max(n for n, it in enumerate(items) if it[0] == kind)

        def move_out(eng, kind, j, n, copy, done):
            b = bank[n % 8]
            if kind == "K":
                eng.wait_ge(S["bd_zero"], 1)
                src = b[:, 0:256].rearrange("p (b k) -> p b k", b=BATCH)
                copy(bd[0:DC, :, 0, :], src[0:DC])
                copy(bd[DC:P, :, 1, :], src[DC:P]).then_inc(done, 1)
            if kind == "D":
                copy(d_sb[0:QP, 4 * j:4 * j + 4, :, :],
                     b[0:QP, :].rearrange("p (h c d) -> p h c d", h=4, c=QC)).then_inc(done, 1)
            if kind == "E":
                copy(e_sb[:, 8 * j:8 * j + 8, :], b[:, :].rearrange("p (h d) -> p h d", h=8)).then_inc(done, 1)
            if kind == "C":
                copy(c_sb[:, 2 * j:2 * j + 2, :], b[:, :].rearrange("p (a m) -> p a m", a=2)).then_inc(done, 1)
            if kind == "F":
                copy(f_sb[:, 2 * j:2 * j + 2, :], b[:, :].rearrange("p (a m) -> p a m", a=2)).then_inc(done, 1)
            if kind == "H":
                copy(hnT[:, :, 2 * j * P:(2 * j + 2) * P],
                     b[:, :].rearrange("p (c m) -> p c m", c=CH)).then_inc(done, 1)
            if kind == "G":
                copy(g_sb[:, j % 2, :, j // 2, :], b[:, :].rearrange("p (b k) -> p b k", b=BATCH)).then_inc(done, 1)
            if kind == "V":
                copy(v_sb[:, 2 * (j % 2):2 * (j % 2) + 2, j // 2, :],
                     b[:, :].rearrange("p (b m) -> p b m", b=2)).then_inc(done, 1)

        def exp_scores(act, t):
            act.wait_ge(S["sc_free"], t + 1)
            if t >= 2:
                act.wait_ge(S["pt"], 2 * (t - 1))
            nc.scalar.activation(p_sb[:, t % 2, :], sc_sb[:, t % 2, :], ACT.Exp).then_inc(S["expd"], 1)

        def turned_out(act, n):
            i, c, hf = n // 4, (n % 4) // 2, n % 2
            act.wait_ge(S["tr"], n + 1)
            if i >= 2:
                act.wait_ge(S["gu"], 4 * (i - 1))
            dst = xt[i % 2][:, c, :, :].rearrange("p g (a b) -> p a g b", b=SLOT_LO)[:, 4 * hf:4 * hf + 4]
            nc.scalar.activation(dst, bank[n % 2][:, :].rearrange("p (a g b) -> p a g b", a=4, b=SLOT_LO),
                                 ACT.Copy).then_inc(S["xt_ok"], 1)

        def y_out(dve, n):
            dve.wait_ge(S["dn"], n + 1)
            if n >= YS:
                dve.wait_ge(s_yw[n % YS], 16 * (n // YS))
            nc.vector.tensor_copy(ysb[n % YS], bank[4 + n % 2][:, :].rearrange("p (q m) -> p q m", q=2)
                                  ).then_inc(S["y_ok"], 1)

        @block.sync
        def _(sp):
            sp.dma_start(ctx_sb[:, :, :], a["ctx"]).then_inc(S["ld_ctx"], 16)
            sp.dma_start(const[:, :], a["const"]).then_inc(S["ld_const"], 16)
            sp.dma_start(wqr[0:RK, :, :], a["wqr"]).then_inc(S["ld_wqr"], 16)
            sp.dma_start(wkr[0:RK, :, :], a["wkr"]).then_inc(S["ld_wqr"], 16)
            sp.dma_start(wkcq[0:QP, :, :, :], a["wkcq"]).then_inc(S["ld_wkcq"], 16)
            sp.dma_start(x[:, :, :], a["x"].rearrange("(t p) m -> p t m", p=P)).then_inc(S["ld_x"], 16)
            sp.dma_start(wq[:, :, :], a["wq"]).then_inc(S["ld_wq"], 16)
            sp.dma_start(wkv[:, :, :], a["wkv"]).then_inc(S["ld_wkv"], 16)
            sp.dma_start(wo[:, :, :], a["wo"]).then_inc(S["ld_wo"], 16)
            sp.dma_start(rw[:, :, :], a["rw"]).then_inc(S["ld_router"], 16)
            sp.dma_start(ebias, a["ebias"]).then_inc(S["ld_router"], 16)
            sp.dma_start(shw[:, :, :], a["shw"]).then_inc(S["ld_sh"], 16)

            def load_group(i):
                s = i % WSLOTS
                sp.dma_start(wgu_sb[s], a["wgu"][i, :, :]).then_inc(s_w[s], 16)
                sp.dma_start(wdn_sb[s][0:FF], a["wdn"][i, :, :]).then_inc(s_w[s], 16)
            sp.wait_ge(S["prep_mm"], NI)
            sp.dma_start(shd[0:FF, :], a["shd"]).then_inc(S["ld_sh"], 16)
            load_group(0)
            load_group(1)
            for t in range(TILES):
                sp.wait_ge(S["hn2"], t + 1)
                sp.dma_start(xn_table[t * P:(t + 1) * P, :], hn[:, t, :]).then_inc(S["xn_wr"], 16)
            sp.wait_ge(S["idx_mm"], 1)
            load_group(2)
            for i in range(GRP):
                for pr in range(4):
                    n = 4 * i + pr
                    sp.wait_ge(S["y_ok"], n + 1)
                    dst = y_table.rearrange("(g i s) m -> i s g m", g=GRP, i=EPG)[i, :, 2 * pr:2 * pr + 2, :]
                    sp.dma_start(dst, ysb[n % YS]).then_inc(s_yw[n % YS], 16)
                if i + WSLOTS < GRP:
                    load_group(i + WSLOTS)
            for t in range(TILES):
                sp.wait_ge(S["added"], TOPK * (t + 1))
                sp.dma_start(out[t * P:(t + 1) * P, :], x[:, t, :]).then_inc(S["outd"], 16)
            sp.wait_ge(S["outd"], 16 * TILES)

        @block.tensor
        def _(pe):
            mm, tr = nc.tensor.matmul, nc.tensor.transpose

            def settle(n):
                act, dve = out_by(n)
                pe.wait_ge(S["prep_act"], act)
                if dve:
                    pe.wait_ge(S["prep_dve"], dve)
            pe.wait_ge(S["ld_const"], 16)
            seen = set()
            for n, (kind, j) in enumerate(items):
                b = bank[n % 8]
                if n >= 8:
                    settle(n - 8)
                first = kind not in seen
                seen.add(kind)
                if kind == "K":
                    pe.wait_ge(S["ctx_roped"], 1)
                    for c in range(2):
                        last = tr(b[:, c * P:(c + 1) * P], kvr[:, c, :], ident)
                if kind == "D":
                    if first:
                        pe.wait_ge(S["ld_wqr"], 32)
                    for q in range(4):
                        for c in range(QC):
                            h = 4 * j + q
                            o = (q * QC + c) * DC
                            last = mm(b[0:QP, o:o + DC], wqr[0:RK, h, c * QP:(c + 1) * QP],
                                      wkr[0:RK, h, :], start=True, stop=True)
                if kind == "E":
                    if first:
                        pe.wait_ge(S["ld_wkcq"], 16)
                        settle(last_of("D"))
                    for q in range(8):
                        h = 8 * j + q
                        for c in range(QC):
                            last = mm(b[:, q * DC:(q + 1) * DC], wkcq[0:QP, h, c, :], d_sb[0:QP, h, c, :],
                                      start=(c == 0), stop=(c == QC - 1))
                if kind == "C":
                    if first:
                        pe.wait_ge(S["ld_wq"], 16)
                        settle(last_of("E"))
                    for q in range(2):
                        for h2 in range(2):
                            h = 4 * j + 2 * q + h2
                            last = mm(b[h2 * DC:(h2 + 1) * DC, q * DIM:(q + 1) * DIM], e_sb[:, h, :], wq[:, h, :],
                                      start=True, stop=True)
                if kind == "F":
                    if first:
                        pe.wait_ge(S["ld_wkv"], 16)
                        pe.wait_ge(S["ld_wo"], 16)
                    for q in range(2):
                        for h2 in range(2):
                            h = 4 * j + 2 * q + h2
                            last = mm(b[h2 * DC:(h2 + 1) * DC, q * DIM:(q + 1) * DIM], wkv[:, h, :], wo[:, h, :],
                                      start=True, stop=True)
                if kind == "H":
                    pe.wait_ge(S["hn1"], 2 * j + 2)
                    for q in range(2):
                        for c in range(CH):
                            o = (c * 2 + q) * P
                            last = tr(b[:, o:o + P], hn[:, 2 * j + q, c * P:(c + 1) * P], ident)
                if kind == "G":
                    if first:
                        settle(last_of("C"))
                    p, c = j // 2, j % 2
                    last = mm(b[:, :], c_sb[:, p, c * P:(c + 1) * P],
                              bd[:, :, :, :].rearrange("p b h k -> p (b h k)"), start=True, stop=True)
                if kind == "V":
                    if first:
                        settle(last_of("F"))
                    p, bp = j // 2, j % 2
                    for q in range(2):
                        last = mm(b[:, q * DIM:(q + 1) * DIM],
                                  bd[:, 2 * bp + q, :, :].rearrange("p h k -> p (h k)"),
                                  f_sb[:, p, :], start=True, stop=True)
                last.then_inc(S["prep_mm"], 1)

            settle(NI - 1)

            def scores(t):
                if t >= 2:
                    pe.wait_ge(S["sc_free"], t - 1)
                for half in range(2):
                    for c in range(CH):
                        last = mm(bank[2 * (t % 2) + half][:, :], hnT[:, c, t * P:(t + 1) * P],
                                  g_sb[:, c, t // TPB, 4 * half:4 * half + 4, :].rearrange("p a b -> p (a b)"),
                                  start=(c == 0), stop=(c == CH - 1))
                last.then_inc(S["scores"], 1)

            def turn_probs(t):
                pe.wait_ge(S["probs"], t + 1)
                if t:
                    pe.wait_ge(S["pt_sb"], 2 * t)
                for half in range(2):
                    for q in range(4):
                        p = 4 * half + q
                        last = tr(bank[4 + half][:, q * P:(q + 1) * P], p_sb[:, t % 2, p * P:(p + 1) * P], ident)
                    last.then_inc(S["pt"], 1)

            def attend(t):
                if t:
                    pe.wait_ge(S["x_ok"], t)
                for p in range(PAIRS):
                    if p % 4 == 0:
                        pe.wait_ge(S["pt_sb"], 2 * t + 1 + p // 4)
                    last = mm(bank[6][:, 0:DIM], pt_sb[:, t % 2, p, :], v_sb[:, t // TPB, p, :],
                              start=(p == 0), stop=(p == PAIRS - 1))
                last.then_inc(S["attn"], 1)

            def turn_hn2(t):
                pe.wait_ge(S["hn2"], t + 1)
                if t:
                    pe.wait_ge(S["hn2T_sb"], t)
                if t % RT == 0 and t:
                    pe.wait_ge(S["elog"], t // RT)
                if t >= 3 and t % RT == 1:
                    pe.wait_ge(S["slot_read"], (t - 1) // RT)
                for c in range(CH):
                    last = tr(bank[7][:, c * P:(c + 1) * P], hn[:, t, c * P:(c + 1) * P], ident)
                last.then_inc(S["hn2T"], 1)

            def route_logits(t):
                pe.wait_ge(S["hn2T_sb"], t + 1)
                if t == 0:
                    pe.wait_ge(S["ld_router"], 32)
                if t % RT == 0 and t:
                    pe.wait_ge(S["elog"], t // RT)
                o = 256 + (t % RT) * EXP
                for c in range(CH):
                    last = mm(bank[7][:, o:o + EXP], hnT[:, c, t * P:(t + 1) * P], rw[:, c, :],
                              start=(c == 0), stop=(c == CH - 1))
                last.then_inc(S["logits"], 1)

            def slot_numbers(k):
                pe.wait_ge(S["pick"], k + 1)
                if k:
                    pe.wait_ge(S["base"], k)
                    pe.wait_ge(S["slot_read"], k)
                if RT * k + 3 < TILES:
                    pe.wait_ge(S["hn2T_sb"], RT * k + 3)
                for r in range(RT):
                    t = RT * k + r
                    o = 384 + r * EXP
                    mm(bank[7][:, o:o + EXP], tri16[:, :], pick16[:, t, :], start=True, stop=False)
                    for q in range(r):
                        mm(bank[7][:, o:o + EXP], ones16[:, :], pick16[:, RT * k + q, :], start=False, stop=False)
                    last = mm(bank[7][:, o:o + EXP], ones16[:, :], base16[:, k, :], start=False, stop=True)
                last.then_inc(S["slotnum"], 1)

            scores(0)
            for t in range(TILES + 1):
                if t + 1 < TILES:
                    scores(t + 1)
                if t < TILES:
                    turn_probs(t)
                if t >= 1:
                    turn_hn2(t - 1)
                if t < TILES:
                    attend(t)
                if t >= 1:
                    route_logits(t - 1)
                if t >= 3 and t % 2 == 1:
                    slot_numbers((t - 3) // 2)

            pe.wait_ge(S["ld_sh"], 32)
            pe.wait_ge(S["sc_free"], TILES)
            for half in range(2):
                for gu in range(2):
                    for c in range(CH):
                        last = mm(bank[2 * half + gu][0:FF, :], shw[:, gu * CH + c, :],
                                  hnT[:, c, half * 512:(half + 1) * 512], start=(c == 0), stop=(c == CH - 1))
                last.then_inc(S["sh_gu"], 1)
            slot_numbers(CHUNKS - 1)

            pe.wait_ge(S["onehot"], TILES)
            for g in range(GRP):
                for t in range(TILES):
                    last = mm(bank[4 + g // 4][0:EXP, (g % 4) * P:(g % 4 + 1) * P],
                              hi_oh[:, t, g * EPG:(g + 1) * EPG, :].rearrange("p e a -> p (e a)"),
                              lo_oh[:, t, g * EPG:(g + 1) * EPG, :].rearrange("p e b -> p (e b)"),
                              start=(t == 0), stop=(t == TILES - 1))
            last.then_inc(S["idx_mm"], 1)
            pe.wait_ge(S["idx_dve"], 2)
            tr(bank[7][:, 0:EXP], idx_p[0:EXP, :], ident[0:EXP, 0:EXP]).then_inc(S["idx_tr"], 1)
            for t in range(TILES):
                if t % 4 == 0:
                    pe.wait_ge(S["sh_h"], t // 4 + 1)
                b = bank[(4, 5, 2, 3)[t // 2]]
                last = mm(b[:, (t % 2) * DIM:(t % 2 + 1) * DIM], h_sh[0:FF, t * P:(t + 1) * P], shd[0:FF, :],
                          start=True, stop=True)
                if t % 2:
                    last.then_inc(S["sh_dn"], 1)

            def turn_tokens(i):
                pe.wait_ge(s_xg[i % 2], 16 * EPG * (i // 2 + 1))
                for c in range(CH):
                    for hf in range(2):
                        n = 4 * i + 2 * c + hf
                        if n >= 2:
                            pe.wait_ge(S["xt_ok"], n - 1)
                        for q in range(4):
                            hi = 4 * hf + q
                            last = tr(bank[n % 2][:, q * P:(q + 1) * P], xg[i % 2][:, hi, c * P:(c + 1) * P], ident)
                        last.then_inc(S["tr"], 1)

            def gate_up(i, pr):
                n = 4 * i + pr
                if pr == 0:
                    pe.wait_ge(s_w[i % WSLOTS], 32 * (i // WSLOTS + 1))
                    pe.wait_ge(S["xt_ok"], 4 * i + 4)
                if n >= 2:
                    pe.wait_ge(S["h"], n - 1)
                w = wgu_sb[i % WSLOTS]
                for q in range(2):
                    g = 2 * pr + q
                    for gu in range(2):
                        o = gu * 256 + q * CAP
                        for c in range(CH):
                            last = mm(bank[2 + n % 2][0:FF, o:o + CAP], w[:, g, gu * CH + c, :],
                                      xt[i % 2][:, c, g, :], start=(c == 0), stop=(c == CH - 1))
                last.then_inc(S["gu"], 1)

            def down(i, pr):
                n = 4 * i + pr
                pe.wait_ge(S["h"], n + 1)
                if n >= 2:
                    pe.wait_ge(S["y_ok"], n - 1)
                for q in range(2):
                    last = mm(bank[4 + n % 2][:, q * DIM:(q + 1) * DIM], ht[n % 2][0:FF, q, :],
                              wdn_sb[i % WSLOTS][0:FF, 2 * pr + q, :], start=True, stop=True)
                last.then_inc(S["dn"], 1)

            pe.wait_ge(S["sh_added"], TILES // 2)
            turn_tokens(0)
            for i in range(GRP):
                for pr in range(4):
                    gate_up(i, pr)
                    if 4 * i + pr:
                        down(i - (pr == 0), (pr - 1) % 4)
                    if pr == 1 and i + 1 < GRP:
                        turn_tokens(i + 1)
            down(GRP - 1, 3)

        @block.scalar
        def _(act):
            A = nc.scalar.activation
            for n, (kind, j) in enumerate(items):
                if n % 2 == 0:
                    act.wait_ge(S["prep_mm"], n + 1)
                    move_out(act, kind, j, n, lambda o, i: A(o, i, ACT.Copy), S["prep_act"])
            for t in range(TILES + 1):
                if t < TILES:
                    if t == 0:
                        exp_scores(act, 0)
                    if t + 1 < TILES:
                        exp_scores(act, t + 1)
                    for half in range(2):
                        act.wait_ge(S["pt"], 2 * t + half + 1)
                        if t >= 2:
                            act.wait_ge(S["attn"], t - 1)
                        A(pt_sb[:, t % 2, 4 * half:4 * half + 4, :],
                          bank[4 + half][:, :].rearrange("p (a b) -> p a b", b=P), ACT.Copy).then_inc(S["pt_sb"], 1)
                if t >= 1:
                    act.wait_ge(S["hn2T"], t)
                    if t == 1:
                        act.wait_ge(S["scores"], TILES if TILES < 2 else 2)
                    A(hnT[:, :, (t - 1) * P:t * P], bank[7][:, 0:DIM].rearrange("p (c q) -> p c q", c=CH),
                      ACT.Copy).then_inc(S["hn2T_sb"], 1)
                    if (t - 1) % RT == RT - 1:
                        act.wait_ge(S["logits"], t)
                        k = (t - 1) // RT
                        if k:
                            act.wait_ge(S["pick"], k)
                        A(el, bank[7][:, 256:384].rearrange("p (r e) -> p r e", r=RT), ACT.Exp,
                          scale=-1.0).then_inc(S["elog"], 1)
            for half in range(2):
                act.wait_ge(S["sh_gu"], half + 1)
                if half:
                    act.wait_ge(S["sh_h"], half)
                A(sg_sh[0:FF, :], bank[2 * half][0:FF, :], ACT.Silu).then_inc(S["sh_act"], 1)
            for i in range(GRP):
                for pr in range(4):
                    if i == 0 and pr == 0:
                        for n in range(4):
                            turned_out(act, n)
                    n = 4 * i + pr
                    act.wait_ge(S["gu"], n + 1)
                    if n >= 2:
                        act.wait_ge(S["h"], n - 1)
                    A(sg[n % 2][0:FF, :, :], bank[2 + n % 2][0:FF, 0:256].rearrange("p (q s) -> p q s", q=2),
                      ACT.Silu).then_inc(S["silu"], 1)
                    if pr == 1 and i + 1 < GRP:
                        for q in range(4):
                            turned_out(act, 4 * (i + 1) + q)

        @block.vector
        def _(dve):
            V = nc.vector
            n_chain = [0]

            def then(ins):
                n_chain[0] += 1
                ins.then_inc(S["d_chain"], 1)
                dve.wait_ge(S["d_chain"], n_chain[0])

            V.memset(bd[:, :, :, :], 0.0).then_inc(S["bd_zero"], 1)
            V.memset(neghalf, -0.5)
            V.memset(base16[:, 0, :], 0.0)
            V.memset(ones16[:, :], 1.0)
            V.memset(gpad, BIG).then_inc(S["small_ok"], 1)
            dve.wait_ge(S["small_ok"], 1)
            dve.wait_ge(S["ld_ctx"], 16)
            dve.wait_ge(S["ld_const"], 16)
            V.tensor_copy(tri16[:, :], const[:, C_TRI:C_TRI + P])
            cosv, sinv = const[:, C_COS:C_COS + DC], const[:, C_SIN:C_SIN + DC]
            hd = DC // 2
            for c in range(2):
                V.tensor_tensor(kvt[:, c, 0:hd], ctx_sb[:, c, hd:DC], sinv[:, 0:hd], ALU.mult)
                V.tensor_tensor(kvt[:, c, hd:DC], ctx_sb[:, c, 0:hd], sinv[:, hd:DC], ALU.mult)
                then(V.tensor_tensor(kvr[:, c, 0:DC], ctx_sb[:, c, :], cosv, ALU.mult))
                then(V.tensor_tensor(kvr[:, c, 0:DC], kvr[:, c, 0:DC], kvt[:, c, :], ALU.add))
                last = V.tensor_copy(kvr[:, c, DC:2 * DC], kvr[:, c, 0:DC])
            last.then_inc(S["ctx_roped"], 1)

            def ln_stats(t):
                then(V.bn_stats(stats[:, t, :], x[:, t, :]))
                return V.bn_aggr(mv[:, t, :], stats[:, t, :])

            def first_norm():
                dve.wait_ge(S["ld_x"], 16)
                for t in range(TILES):
                    last = ln_stats(t)
                last.then_inc(S["stats1"], 1)
                dve.wait_ge(S["rstd1"], 1)
                for t in range(TILES):
                    V.tensor_scalar(hn[:, t, :], x[:, t, :], mv[:, t, 0:1], rstd[:, t:t + 1],
                                    ALU.subtract, ALU.mult).then_inc(S["hn1"], 1)

            for n, (kind, j) in enumerate(items):
                if n == 5:
                    first_norm()
                if n % 2 == 1:
                    dve.wait_ge(S["prep_mm"], n + 1)
                    move_out(dve, kind, j, n, V.tensor_copy, S["prep_dve"])

            def soften(t):
                dve.wait_ge(S["scores"], t + 1)
                for half in range(2):
                    ins = V.reduce_max(rmax[:, t % 2, 8 * half:8 * half + 8],
                                       bank[2 * (t % 2) + half][:, :].rearrange("p (h k) -> p h k", h=8), AX.X)
                then(ins)
                if t >= 2:
                    dve.wait_ge(S["expd"], t - 1)
                for half in range(2):
                    last = V.tensor_tensor(
                        sc_sb[:, t % 2, 512 * half:512 * half + 512].rearrange("p (h k) -> p h k", h=8),
                        bank[2 * (t % 2) + half][:, :].rearrange("p (h k) -> p h k", h=8),
                        rmax[:, t % 2, 8 * half:8 * half + 8].unsqueeze(2).to_broadcast([P, 8, KEYS]), ALU.subtract)
                last.then_inc(S["sc_free"], 1)

            def sum_probs(t):
                dve.wait_ge(S["expd"], t + 1)
                if t >= 2:
                    dve.wait_ge(S["probs"], t - 1)
                then(V.reduce_sum(rsum[:, t % 2, :], p_sb[:, t % 2, :].rearrange("p (h k) -> p h k", h=HEADS), AX.X))
                V.reciprocal(rsum[:, t % 2, :], rsum[:, t % 2, :]).then_inc(S["rsum_ok"], 1)

            def add_attn(t):
                dve.wait_ge(S["attn"], t + 1)
                V.tensor_tensor(x[:, t, :], x[:, t, :], bank[6][:, 0:DIM], ALU.add).then_inc(S["x_ok"], 1)
                dve.wait_ge(S["x_ok"], t + 1)
                ln_stats(t).then_inc(S["stats2"], 1)

            def second_norm(t):
                dve.wait_ge(S["rstd2"], t + 1)
                V.tensor_scalar(hn[:, t, :], x[:, t, :], mv[:, t, 0:1], rstd[:, t:t + 1],
                                ALU.subtract, ALU.mult).then_inc(S["hn2"], 1)

            def pick_experts(k):
                dve.wait_ge(S["elog"], k + 1)
                then(V.tensor_scalar_add(s0, el, 1.0))
                then(V.reciprocal(s0, s0))
                then(V.tensor_tensor(sc, s0, ebias.unsqueeze(1).to_broadcast([P, RT, EXP]), ALU.add))
                g = sc.rearrange("p r (g e) -> p r g e", g=GRP)
                V.tensor_tensor(m1, g[:, :, :, 0:4], g[:, :, :, 4:8], ALU.max)
                then(V.tensor_tensor(n1, g[:, :, :, 0:4], g[:, :, :, 4:8], ALU.min))
                V.tensor_tensor(m2, m1[:, :, :, 0:2], m1[:, :, :, 2:4], ALU.max)
                V.tensor_tensor(t2, m1[:, :, :, 0:2], m1[:, :, :, 2:4], ALU.min)
                then(V.tensor_tensor(n2, n1[:, :, :, 0:2], n1[:, :, :, 2:4], ALU.max))
                then(V.tensor_tensor(n2, n2, t2, ALU.max))
                V.tensor_tensor(gs, m2[:, :, :, 0], m2[:, :, :, 1], ALU.max)
                V.tensor_tensor(t3, m2[:, :, :, 0], m2[:, :, :, 1], ALU.min)
                then(V.tensor_tensor(n3, n2[:, :, :, 0], n2[:, :, :, 1], ALU.max))
                then(V.tensor_tensor(n3, n3, t3, ALU.max))
                then(V.tensor_tensor(gpad[:, :, 0:GRP], gs, n3, ALU.add))
                for r in range(RT):
                    ins = V.max(top4[:, r, :], gpad[:, r, 0:GRP])
                then(ins)
                then(V.memset(top4[:, :, TOPG:8], BIG))
                for r in range(RT):
                    ins = V.match_replace(rep[:, r, 0:16], top4[:, r, :], gpad[:, r, :], -BIG)
                then(ins)
                then(V.tensor_single_scalar(gpick, rep[:, :, 0:GRP], -BIG, ALU.is_equal))
                then(V.tensor_tensor(msk.rearrange("p r (g e) -> p r g e", g=GRP), g,
                                     gpick.unsqueeze(3).to_broadcast([P, RT, GRP, EPG]), ALU.mult))
                for r in range(RT):
                    ins = V.max(top8[:, r, :], msk[:, r, :])
                then(ins)
                for r in range(RT):
                    ins = V.match_replace(rep[:, r, :], top8[:, r, :], msk[:, r, :], -BIG)
                then(ins)
                V.tensor_single_scalar(pick16[:, RT * k:RT * k + RT, :], rep, -BIG, ALU.is_equal).then_inc(S["pick"], 1)
                dve.wait_ge(S["pick"], k + 1)
                if k + 1 < CHUNKS:
                    then(V.tensor_tensor(base16[:, k + 1, :], base16[:, k, :], pick16[:, RT * k, :], ALU.add))
                    V.tensor_tensor(base16[:, k + 1, :], base16[:, k + 1, :], pick16[:, RT * k + 1, :],
                                    ALU.add).then_inc(S["base"], 1)
                for r in range(RT):
                    t = RT * k + r
                    ins = V.scalar_tensor_tensor(wsel[:, t, :], s0[:, r, :], 1.0, pick16[:, t, :], ALU.mult, ALU.mult,
                                                 accum_out=wsum[:, t:t + 1])
                then(ins)

            def place_experts(k):
                dve.wait_ge(S["slotnum"], k + 1)
                ts = slice(RT * k, RT * k + RT)
                V.scalar_tensor_tensor(slot_i[:, :, :], pick16[:, ts, :], -UNPICKED,
                                       bank[7][:, 384:512].rearrange("p (r e) -> p r e", r=RT),
                                       ALU.mult, ALU.add).then_inc(S["slot_read"], 1)
                dve.wait_ge(S["slot_read"], k + 1)
                V.tensor_single_scalar(hi_i[:, :, :], slot_i[:, :, :], 4, ALU.arith_shift_right)
                then(V.tensor_single_scalar(lo_i[:, :, :], slot_i[:, :, :], SLOT_LO - 1, ALU.bitwise_and))
                for r in range(RT):
                    t = RT * k + r
                    V.tensor_tensor(lo_oh[:, t, :, :], lo_i[:, r, :].unsqueeze(2).to_broadcast([P, EXP, SLOT_LO]),
                                    const[:, C_LO:C_LO + SLOT_LO].unsqueeze(1).to_broadcast([P, EXP, SLOT_LO]),
                                    ALU.is_equal)
                    ins = V.tensor_tensor(hi_oh[:, t, :, :], hi_i[:, r, :].unsqueeze(2).to_broadcast([P, EXP, SLOT_HI]),
                                          const[:, C_HI:C_HI + SLOT_HI].unsqueeze(1).to_broadcast([P, EXP, SLOT_HI]),
                                          ALU.is_equal)
                then(ins)
                for r in range(RT):
                    t = RT * k + r
                    V.tensor_scalar(hi_oh[:, t, :, :], hi_oh[:, t, :, :], const[:, C_TOK + t:C_TOK + t + 1], None,
                                    ALU.mult).then_inc(S["onehot"], 1)
                then(V.tensor_tensor(key1, slot_i[:, :, :],
                                     const[:, C_KEY:C_KEY + EXP].unsqueeze(1).to_broadcast([P, RT, EXP]), ALU.add))
                V.scalar_tensor_tensor(keys[:, ts, :], slot_i[:, :, :], FAR, key1, ALU.is_lt, ALU.mult)
                then(V.scalar_tensor_tensor(wsel[:, ts, :], slot_i[:, :, :], FAR, wsel[:, ts, :], ALU.is_lt, ALU.mult))

            soften(0)
            sum_probs(0)
            for t in range(TILES + 3):
                if t + 1 < TILES:
                    soften(t + 1)
                if t >= 3 and t % 2 == 1 and (t - 3) // 2 < CHUNKS:
                    pick_experts((t - 3) // 2)
                if t >= 4 and t % 2 == 0 and (t - 4) // 2 < CHUNKS:
                    place_experts((t - 4) // 2)
                if t + 1 < TILES:
                    sum_probs(t + 1)
                if t < TILES:
                    add_attn(t)
                    second_norm(t)

            dve.wait_ge(S["idx_mm"], 1)
            for b in range(2):
                ins = V.tensor_tensor(
                    idx_d[:, 4 * b:4 * b + 4, :, :],
                    bank[4 + b][0:EXP, :].rearrange("p (g i b) -> p g i b", g=4, b=SLOT_LO),
                    const[0:EXP, C_DIAG:C_DIAG + EPG].unsqueeze(1).unsqueeze(3).to_broadcast([EXP, 4, EPG, SLOT_LO]),
                    ALU.mult)
            ins.then_inc(S["idx_dve"], 1)
            dve.wait_ge(S["idx_dve"], 1)
            V.reduce_sum(idx_p[0:EXP, :].rearrange("p (g b) -> p g b", b=SLOT_LO),
                         idx_d.rearrange("p g i b -> p g b i"), AX.X).then_inc(S["idx_dve"], 1)
            dve.wait_ge(S["idx_tr"], 1)
            V.tensor_copy(idx_t[:, :], bank[7][:, 0:EXP]).then_inc(S["idx_ok"], 1)

            for half in range(2):
                dve.wait_ge(S["sh_act"], half + 1)
                V.tensor_tensor(h_sh[0:FF, half * 512:(half + 1) * 512], sg_sh[0:FF, :], bank[2 * half + 1][0:FF, :],
                                ALU.mult).then_inc(S["sh_h"], 1)
            for j in range(TILES // 2):
                dve.wait_ge(S["sh_dn"], j + 1)
                b = bank[(4, 5, 2, 3)[j]]
                V.tensor_tensor(x[:, 2 * j:2 * j + 2, :], x[:, 2 * j:2 * j + 2, :],
                                b[:, :].rearrange("p (t m) -> p t m", t=2), ALU.add).then_inc(S["sh_added"], 1)
            then(V.tensor_scalar_add(wsum, wsum, 1e-20))
            then(V.reciprocal(wrec, wsum))

            def weigh(t):
                then(V.max(key8[:, t, :], keys[:, t, :]))
                V.tensor_scalar(rows8[:, t * TOPK:(t + 1) * TOPK], key8[:, t, :], 1.0, 0.0,
                                ALU.subtract, ALU.max).then_inc(S["rows"], 1)
                then(V.tensor_tensor(eq, keys[:, t, :].unsqueeze(1).to_broadcast([P, TOPK, EXP]),
                                     key8[:, t, :].unsqueeze(2).to_broadcast([P, TOPK, EXP]), ALU.is_equal))
                then(V.tensor_tensor(eqw, eq, wsel[:, t, :].unsqueeze(1).to_broadcast([P, TOPK, EXP]), ALU.mult))
                then(V.reduce_sum(wgt8[:, t, :], eqw, AX.X))
                V.tensor_scalar(wgt8[:, t, :], wgt8[:, t, :], wrec[:, t:t + 1], SCALE,
                                ALU.mult, ALU.mult).then_inc(S["wgt"], 1)

            for i in range(GRP):
                for pr in range(4):
                    n = 4 * i + pr
                    dve.wait_ge(S["silu"], n + 1)
                    if n >= 2:
                        dve.wait_ge(S["dn"], n - 1)
                    V.tensor_tensor(ht[n % 2][0:FF, :, :], sg[n % 2][0:FF, :, :],
                                    bank[2 + n % 2][0:FF, 256:512].rearrange("p (q s) -> p q s", q=2),
                                    ALU.mult).then_inc(S["h"], 1)
                    if n:
                        y_out(dve, n - 1)
                    if pr == 0:
                        weigh(i)
            y_out(dve, 4 * GRP - 1)
            dve.wait_ge(S["wgt"], TILES)
            for m in range(TILES * TOPK):
                t, k = m // TOPK, m % TOPK
                dve.wait_ge(s_yg[m % RING], 16 * (m // RING + 1))
                if k:
                    dve.wait_ge(S["added"], m)
                V.scalar_tensor_tensor(x[:, t, :], yg[m % RING], wgt8[:, t, k:k + 1], x[:, t, :],
                                       ALU.mult, ALU.add).then_inc(S["added"], 1)

        @block.gpsimd
        def _(pool):
            G = nc.gpsimd
            n_chain = [0]

            def then(ins):
                n_chain[0] += 1
                ins.then_inc(S["p_chain"], 1)
                pool.wait_ge(S["p_chain"], n_chain[0])

            def rsqrt(ts, n):
                then(G.tensor_scalar_add(veps[:, ts], mv[:, ts, 1], EPS))
                then(G.tensor_tensor(rs0[:, ts], veps[:, ts], neghalf.to_broadcast([P, n]), ALU.pow))
                then(G.tensor_tensor(rs1[:, ts], rs0[:, ts], rs0[:, ts], ALU.mult))
                then(G.tensor_tensor(rs1[:, ts], rs1[:, ts], veps[:, ts], ALU.mult))
                then(G.tensor_scalar(rs1[:, ts], rs1[:, ts], -0.5, 1.5, ALU.mult, ALU.add))
                return G.tensor_tensor(rstd[:, ts], rs0[:, ts], rs1[:, ts], ALU.mult)

            pool.wait_ge(S["small_ok"], 1)
            pool.wait_ge(S["stats1"], 1)
            rsqrt(slice(0, TILES), TILES).then_inc(S["rstd1"], 1)

            def normalise(t):
                pool.wait_ge(S["rsum_ok"], t + 1)
                v = p_sb[:, t % 2, :].rearrange("p (h k) -> p h k", h=HEADS)
                G.tensor_tensor(v, v, rsum[:, t % 2, :].unsqueeze(2).to_broadcast([P, HEADS, KEYS]),
                                ALU.mult).then_inc(S["probs"], 1)

            normalise(0)
            for t in range(TILES):
                if t + 1 < TILES:
                    normalise(t + 1)
                pool.wait_ge(S["stats2"], t + 1)
                rsqrt(slice(t, t + 1), 1).then_inc(S["rstd2"], 1)

            pool.wait_ge(S["idx_ok"], 1)
            pool.wait_ge(S["xn_wr"], 16 * TILES)
            for i in range(GRP):
                if i >= 2:
                    pool.wait_ge(S["tr"], 4 * (i - 1))
                for hi in range(EPG):
                    j = i * EPG + hi
                    G.indirect_dma_start(
                        out=xg[i % 2][:, hi, :], out_offset=None, in_=xn_table[:, :],
                        in_offset=bass.IndirectOffsetOnAxis(ap=idx_t[:, j:j + 1], axis=0)).then_inc(s_xg[i % 2], 16)
            for s in range(YS):
                pool.wait_ge(s_yw[s], 16 * (4 * GRP // YS))
            pool.wait_ge(S["rows"], TILES)
            for m in range(TILES * TOPK):
                if m >= RING:
                    pool.wait_ge(S["added"], m - RING + 1)
                G.indirect_dma_start(
                    out=yg[m % RING], out_offset=None, in_=y_table[:, :],
                    in_offset=bass.IndirectOffsetOnAxis(ap=rows8[:, m:m + 1], axis=0)).then_inc(s_yg[m % RING], 16)


def constants():
    import numpy as np
    c = np.zeros((P, C_ALL), np.float32)
    c[:, C_IDENT:C_IDENT + P] = np.eye(P)
    for i in range(EPG):
        c[i * SLOT_HI:(i + 1) * SLOT_HI, C_DIAG + i] = 1.0
    c[:, C_KEY:C_KEY + EXP] = np.arange(EXP) * CAP + 1 + UNPICKED
    c[:, C_HI:C_HI + SLOT_HI] = np.arange(SLOT_HI) - UNPICKED / SLOT_LO
    c[:, C_LO:C_LO + SLOT_LO] = np.arange(SLOT_LO)
    c[:, C_TOK:C_TOK + TILES] = np.arange(P)[:, None] + P * np.arange(TILES)
    inv = (1.0 / np.float32(10000.0) ** (np.arange(0, DC, 2, dtype=np.float32) / np.float32(DC))).astype(np.float32)
    fr = np.arange(KEYS, dtype=np.float32)[:, None] * inv[None, :]
    cos, sin = np.repeat(np.cos(fr), 2, -1), np.repeat(np.sin(fr), 2, -1)
    sin[:, :DC // 2] *= -1.0
    c[:, C_COS:C_COS + DC] = np.tile(cos, (P // KEYS, 1))
    c[:, C_SIN:C_SIN + DC] = np.tile(sin, (P // KEYS, 1))
    c[:, C_TRI:C_TRI + P] = np.triu(np.ones((P, P)), 1)
    return c


def kernel(**inputs):
    import numpy as np
    import concourse.bacc as bacc
    from concourse.bass_utils import run_bass_kernel_spmd

    v = {k.removeprefix("L0_"): np.asarray(a) for k, a in inputs.items()}

    def pack(w):
        e, r, c = w.shape
        return w.reshape(GRP, EPG, r // P, P, c).transpose(1, 3, 0, 2, 4)
    gate, up = pack(v["ffn_w_gate"]), pack(v["ffn_w_up"])
    d = {
        "x": v["x"].reshape(TOK, DIM),
        "ctx": v["ctx_512"].reshape(2, P, DC).transpose(1, 0, 2),
        "const": constants(),
        "wq": v["xattn_Wq"].reshape(HEADS, HK, DIM).transpose(1, 0, 2),
        "wkcq": v["xattn_w_kc_q"].reshape(HEADS, HK, QC, QP).transpose(3, 0, 2, 1),
        "wqr": v["xattn_W_qr"].transpose(2, 0, 1),
        "wkr": v["xattn_W_kr"].transpose(2, 0, 1),
        "wkv": v["xattn_w_kc_kv"].transpose(1, 0, 2),
        "wo": v["xattn_Wo"].reshape(DIM, HEADS, HK).transpose(2, 1, 0),
        "rw": v["ffn_router_weight"].reshape(EXP, CH, P).transpose(2, 1, 0),
        "ebias": np.tile(v["ffn_e_bias"].reshape(1, EXP), (P, 1)),
        "shw": np.concatenate([v[n].reshape(CH, P, FF).transpose(1, 0, 2) for n in ("ffn_sh_gate", "ffn_sh_up")], 1),
        "shd": v["ffn_sh_down"],
        "wgu": np.concatenate([gate, up], 3).reshape(EPG, P, GRP * 2 * CH * FF),
        "wdn": v["ffn_w_down"].reshape(GRP, EPG, FF, DIM).transpose(1, 2, 0, 3).reshape(EPG, FF, GRP * DIM),
    }
    nc = bacc.Bacc("TRN2", target_bir_lowering=False, num_devices=1)
    arrays, aps = {}, {}
    for name, arr in d.items():
        arr = np.ascontiguousarray(arr)
        arrays[f"in_{name}"] = arr
        aps[name] = nc.dram_tensor(f"in_{name}", arr.shape, mybir.dt.float32, kind="ExternalInput").ap()
    out = nc.dram_tensor("out", (TOK, DIM), mybir.dt.float32, kind="ExternalOutput").ap()
    program(nc, aps, out, None)
    r = run_bass_kernel_spmd(nc, [arrays], core_ids=[0])
    return r.results[0]["out"].reshape(BATCH, SEQ, DIM)
```

```python
import concourse.bass as bass
from concourse import mybir
from contextlib import ExitStack

P = 128
BATCH, SEQ, DIM = 4, 256, 256
TOK = BATCH * SEQ
TILES = TOK // P
TPB = SEQ // P
KEYS, DC = 64, 64
HEADS, HK, DQ, RK = 16, 128, 192, 64
PAIRS = HEADS // 2
QC = 2
QP = DQ // QC
CH = DIM // P
EXP, GRP, EPG = 64, 8, 8
TOPG, TOPK, FF = 4, 8, 88
CAP = 128
SCALE = 2.5
EPS = 1e-5
CHUNKS = [(0, 1), (1, 1), (2, 2), (4, 2), (6, 1), (7, 1)]
NC = len(CHUNKS)
NSUM = 3
BIG = 3.0e38
UNPICKED = 2048.0
FAR = CAP - UNPICKED
ROW = DIM + EXP + 4
C_NUM = DIM + EXP

C_IDENT = 0
C_KEY = C_IDENT + P
C_DUMP = C_KEY + EXP
C_TOK = C_DUMP + 1
C_COS = C_TOK + TILES
C_SIN = C_COS + DC
C_TRI = C_SIN + DC
C_ALL = C_TRI + P


def program(nc, a, out, dbg):
    f32, f16, u32 = mybir.dt.float32, mybir.dt.float16, mybir.dt.uint32
    ALU, ACT, AX = mybir.AluOpType, mybir.ActivationFunctionType, mybir.AxisListType
    ctx = ExitStack()
    with ctx:
        def sb(name, shape, dt=f32):
            return ctx.enter_context(nc.sbuf_tensor(name, shape, dt))

        def sem(name):
            return ctx.enter_context(nc.semaphore(name))

        xe_table = nc.dram_tensor("xe_table", (EXP * CAP, ROW), f32, kind="Internal").ap()
        sums = [nc.dram_tensor(f"sums{s}", (TOK + CAP, DIM), f32, kind="Internal").ap() for s in range(NSUM)]

        const = sb("const", [P, C_ALL])
        x = sb("x", [P, TILES, DIM])
        hn = sb("hn", [P, TILES, ROW])
        hnT = sb("hnT", [P, CH, TOK])
        bd = sb("bd", [P, BATCH, 2, KEYS])
        g_sb = sb("g_sb", [P, CH, BATCH, PAIRS, P])
        v_sb = sb("v_sb", [P, BATCH, PAIRS, DIM])
        region = sb("region", [P, 26624])
        small = sb("small", [P, 2048])
        tri16 = sb("tri16", [P, P], f16)
        ones16 = sb("ones16", [P, P], f16)

        def view(base, off, *dims):
            n = 1
            for d in dims:
                n *= d
            ap = base[:, off:off + n]
            if len(dims) == 2:
                ap = ap.rearrange("p (a b) -> p a b", b=dims[1])
            if len(dims) == 3:
                ap = ap.rearrange("p (a b c) -> p a b c", b=dims[1], c=dims[2])
            if len(dims) == 4:
                ap = ap.rearrange("p (a b c d) -> p a b c d", b=dims[1], c=dims[2], d=dims[3])
            return ap

        wkcq = view(region, 0, HEADS, QC, HK)
        wqr = view(region, 4096, HEADS, QC, RK)
        wkr = view(region, 6144, PAIRS, DC)
        a_sb = view(region, 8192, PAIRS, HK)
        e_sb = view(region, 10240, HEADS, DC)
        wkv = view(region, 11264, HEADS, DC)
        wq = view(region, 12288, HEADS, DIM)
        wo = view(region, 16384, HEADS, DIM)
        c_sb = view(region, 20480, PAIRS, DIM)
        f_sb = view(region, 22528, PAIRS, DIM)
        ctx_sb = view(region, 24576, 2, DC)
        kvr = view(region, 24704, 2, 2 * DC)
        kvt = view(region, 24960, 2, DC)
        p_sb = view(region, 2048, 2, HEADS * KEYS)
        pt_sb = view(region, 4096, 2, PAIRS, P)
        WG = EPG * CH * 2 * FF
        WD = EPG * DIM
        WSLOTS = 4
        w_at = [12288, 12288 + WG + WD, 0, WG + WD]
        wgu_sb = [view(region, o, EPG, CH, 2 * FF) for o in w_at]
        wdn_sb = [view(region, o + WG, EPG, DIM) for o in w_at]
        h_sh = view(region, 22016, TOK)
        empty = view(region, 26240 - ROW, ROW)
        zeros = view(region, 26240, DIM)
        g_flat = g_sb[:, :, :, :, :].rearrange("p a b c d -> p (a b c d)")
        v_flat = v_sb[:, :, :, :].rearrange("p a b c -> p (a b c)")
        XS = 3
        xe = [view(g_flat, s * GRP * ROW, GRP, ROW) for s in range(XS)]
        xt = [view(v_flat, s * 512, 2, CH, CAP) for s in range(2)]
        sg = [view(v_flat, 1024 + s * 256, 2, FF) for s in range(2)]
        hw = [view(v_flat, 1536 + s * 256, 2, FF) for s in range(2)]
        ht = [view(v_flat, 2048 + s * 256, 2, CAP) for s in range(2)]
        YS = 4
        ysb = [view(v_flat, 2560 + s * 512, 2, DIM) for s in range(YS)]
        sg_sh = view(v_flat, 4608, 512)
        acc = [view(g_flat, 0, TILES, DIM), view(g_flat, 2048, TILES, DIM), view(g_flat, 4096, TILES, DIM)]

        at = [0]

        def take(*dims):
            n = 1
            for d in dims:
                n *= d
            v = view(small, at[0], *dims)
            at[0] += n
            return v
        rmax, rsum = take(2, HEADS), take(2, HEADS)
        stats, mv = take(TILES, 6), take(TILES, 2)
        veps, lnv, rs0, rs1, rstd = take(TILES), take(TILES), take(TILES), take(TILES), take(TILES)
        ebias = take(EXP)
        el, s0, sc = take(2, EXP), take(2, EXP), take(2, EXP)
        m1, n1 = take(2, GRP, 4), take(2, GRP, 4)
        m2, n2, t2 = take(2, GRP, 2), take(2, GRP, 2), take(2, GRP, 2)
        gs, n3, t3 = take(2, GRP), take(2, GRP), take(2, GRP)
        top4 = take(2, 8)
        gpad = take(2, 16)
        gpick = take(2, GRP)
        msk, rep = take(2, EXP), take(2, EXP)
        top8 = take(2, 8)
        key8 = take(2, TOPK)
        over = take(2, TOPK)
        wsum = take(TILES)
        slot, key1, keys = take(2, EXP), take(2, EXP), take(2, EXP)
        shw = view(region, 25536, 2 * CH, FF)
        shd = view(region, 24064, DIM)
        rw = view(region, 25216, CH, EXP)
        pick16 = region[:, 24320:24576].bitcast(f16).rearrange("p (t e) -> p t e", e=EXP)
        base16 = region[:, 25344:25536].bitcast(f16).rearrange("p (k e) -> p k e", e=EXP)
        rows8 = sb("rows8", [P, TILES * TOPK], u32)
        ident = const[:, C_IDENT:C_IDENT + P]

        bank = [ctx.enter_context(nc.psum_tensor(f"bank{i}", [P, 512], f32)) for i in range(8)]

        DVE_PICKS = {first + n + 1: k for k, (first, n) in enumerate(CHUNKS)}
        PE_SLOTS = {t + 1: k for t, k in DVE_PICKS.items()}
        names = ("ld_const ld_x ld_ctx ld_wqr0 ld_wqr1 ld_wkr ld_wkcq0 ld_wkcq1 ld_wq ld_wkv ld_wo ld_router ld_sh ld_empty "
                 "filled zeroed ctx_roped bd_zero zero_ok num_ok prep_mm prep_act prep_dve stats1 rstd1 hn1 "
                 "scores nmax expd probs pt pt_sb attn x_ok stats2 rstd2 hn2 "
                 "hn2T hn2T_sb logits elog pick base slotnum slot_read rows weights spread "
                 "sh_gu sh_act sh_h sh_dn sh_added "
                 "tx xt_ok gu silu h th ht_ok dn y_ok "
                 "added outd d_chain a_chain small_ok").split()
        S = {n: sem(n) for n in names}
        s_w = [sem(f"ld_expert{s}") for s in range(WSLOTS)]
        s_xe = [[sem(f"ld_rows{s}_{hf}") for hf in range(2)] for s in range(XS)]
        s_sum = [sem(f"summed{s}") for s in range(NSUM)]
        s_acc = [[sem(f"ld_sums{s}_{hf}") for hf in range(2)] for s in range(NSUM)]

        def sums_after(m, s):
            return 16 * ((m - s + NSUM - 1) // NSUM)

        block = ctx.enter_context(nc.Block())

        TPV = 2 * PAIRS
        items = ([("K", 0)] + [("A", n) for n in range(2)] + [("E", n) for n in range(2)]
                 + [("C", n) for n in range(4)] + [("G", n) for n in range(8)]
                 + [("H", n) for n in range(4)] + [("G", n) for n in range(8, 16)]
                 + [("F", n) for n in range(4)] + [("V", n) for n in range(TPV)])
        NI = len(items)
        NV = NI - TPV
        bank_of = [n % 8 if n < NV else 4 + (n - NV) % 4 for n in range(NI)]
        by_act = [n < 9 and it[0] != "C" or n % 2 == 0 for n, it in enumerate(items[:NV])]
        by_act += [j % 3 == 0 for j in range(TPV)]

        def out_by(n):
            a = sum(by_act[:n + 1])
            return a, n + 1 - a

        def last_of(kind):
            return max(n for n, it in enumerate(items) if it[0] == kind)

        def move_out(eng, kind, j, n, copy, done):
            b = bank[bank_of[n]]
            if kind == "K":
                eng.wait_ge(S["bd_zero"], 1)
                src = b[:, 0:256].rearrange("p (b k) -> p b k", b=BATCH)
                copy(bd[0:DC, :, 0, :], src[0:DC])
                copy(bd[DC:P, :, 1, :], src[DC:P]).then_inc(done, 1)
            if kind == "A":
                copy(a_sb[:, 4 * j:4 * j + 4, :], b[:, :].rearrange("p (a k) -> p a k", a=4)).then_inc(done, 1)
            if kind == "E":
                copy(e_sb.rearrange("p (a b) d -> p a b d", b=2)[:, :, j, :],
                     b[:, :].rearrange("p (a d) -> p a d", a=PAIRS)).then_inc(done, 1)
            if kind == "C":
                copy(c_sb[:, 2 * j:2 * j + 2, :], b[:, :].rearrange("p (a m) -> p a m", a=2)).then_inc(done, 1)
            if kind == "F":
                copy(f_sb[:, 2 * j:2 * j + 2, :], b[:, :].rearrange("p (a m) -> p a m", a=2)).then_inc(done, 1)
            if kind == "H":
                copy(hnT[:, :, 2 * j * P:(2 * j + 2) * P],
                     b[:, :].rearrange("p (c m) -> p c m", c=CH)).then_inc(done, 1)
            if kind == "G":
                copy(g_sb[:, j % 2, :, j // 2, :], b[:, :].rearrange("p (b k) -> p b k", b=BATCH)).then_inc(done, 1)
            if kind == "V":
                copy(v_sb[:, 2 * (j % 2):2 * (j % 2) + 2, j // 2, :],
                     b[:, :].rearrange("p (b m) -> p b m", b=2)).then_inc(done, 1)

        @block.sync
        def _(sp):
            sp.dma_start(ctx_sb[:, :, :], a["ctx"]).then_inc(S["ld_ctx"], 16)
            sp.dma_start(const[:, :], a["const"]).then_inc(S["ld_const"], 16)
            for j in range(2):
                hs = slice(8 * j, 8 * j + 8)
                sp.dma_start(wqr[0:QP, hs, :, :], a["wqr"][:, hs, :, :]).then_inc(S[f"ld_wqr{j}"], 16)
                sp.dma_start(wkcq[0:QP, hs, :, :], a["wkcq"][:, hs, :, :]).then_inc(S[f"ld_wkcq{j}"], 16)
            sp.dma_start(wkr[:, :, :], a["wkr"]).then_inc(S["ld_wkr"], 16)
            sp.dma_start(x[:, :, :], a["x"].rearrange("(t p) m -> p t m", p=P)).then_inc(S["ld_x"], 16)
            sp.dma_start(wq[:, :, :], a["wq"]).then_inc(S["ld_wq"], 16)
            sp.dma_start(wkv[:, :, :], a["wkv"]).then_inc(S["ld_wkv"], 16)
            sp.dma_start(wo[:, :, :], a["wo"]).then_inc(S["ld_wo"], 16)
            sp.dma_start(rw[:, :, :], a["rw"]).then_inc(S["ld_router"], 16)
            sp.dma_start(ebias, a["ebias"]).then_inc(S["ld_router"], 16)
            sp.dma_start(shw[:, :, :], a["shw"]).then_inc(S["ld_sh"], 16)
            sp.dma_start(empty, a["empty"]).then_inc(S["ld_empty"], 16)
            sp.wait_ge(S["ld_empty"], 16)
            for i in range(EPG):
                sp.dma_start(xe_table[i * GRP * CAP:(i + 1) * GRP * CAP, :].rearrange("(s g) m -> s g m", g=GRP),
                             empty.unsqueeze(1).to_broadcast([P, GRP, ROW])).then_inc(S["filled"], 16)
            sp.wait_ge(S["zero_ok"], 1)
            for s in range(NSUM):
                sp.dma_start(sums[s].rearrange("(t p) m -> p t m", p=P),
                             zeros.unsqueeze(1).to_broadcast([P, TILES + 1, DIM])).then_inc(S["zeroed"], 16)

            def load_group(i):
                s = i % WSLOTS
                sp.dma_start(wgu_sb[s], a["wgu"][i, :, :]).then_inc(s_w[s], 16)
                sp.dma_start(wdn_sb[s][0:FF], a["wdn"][i, :, :]).then_inc(s_w[s], 16)

            def load_rows(i):
                src = xe_table[i * GRP * CAP:(i + 1) * GRP * CAP, :].rearrange("(s g) m -> s g m", g=GRP)
                for hf in range(2):
                    sp.dma_start(xe[i % XS][:, 4 * hf:4 * hf + 4, :],
                                 src[:, 4 * hf:4 * hf + 4, :]).then_inc(s_xe[i % XS][hf], 16)

            sp.wait_ge(S["prep_mm"], NI)
            sp.dma_start(shd[0:FF, :], a["shd"]).then_inc(S["ld_sh"], 16)
            load_group(0)
            load_group(1)
            sp.wait_ge(S["spread"], 16 * TILES * TOPK)
            load_rows(0)
            load_rows(1)
            load_rows(2)
            load_group(2)
            load_group(3)
            for i in range(GRP - 1):
                sp.wait_ge(S["y_ok"], 4 * i + 4)
                if i + XS < GRP:
                    for s in range(NSUM):
                        sp.wait_ge(s_sum[s], sums_after(GRP * (i + 1), s))
                    load_rows(i + XS)
                if i + WSLOTS < GRP:
                    load_group(i + WSLOTS)
            for s in range(NSUM):
                sp.wait_ge(s_sum[s], sums_after(EXP, s))
            for hf in range(2):
                ts = slice(hf * TILES // 2, (hf + 1) * TILES // 2)
                for s in range(NSUM):
                    sp.dma_start(acc[s][:, ts, :],
                                 sums[s][0:TOK, :].rearrange("(t p) m -> p t m", p=P)[:, ts, :]).then_inc(s_acc[s][hf], 16)
            for hf in range(2):
                ts = slice(hf * TILES // 2, (hf + 1) * TILES // 2)
                sp.wait_ge(S["added"], NSUM * (hf + 1))
                sp.dma_start(out.rearrange("(t p) m -> p t m", p=P)[:, ts, :], x[:, ts, :]).then_inc(S["outd"], 16)
            sp.wait_ge(S["outd"], 32)

        @block.tensor
        def _(pe):
            mm, tr = nc.tensor.matmul, nc.tensor.transpose

            def settle(n):
                act, dve = out_by(n)
                pe.wait_ge(S["prep_act"], act)
                if dve:
                    pe.wait_ge(S["prep_dve"], dve)
            def scores(t):
                if t >= 2:
                    pe.wait_ge(S["expd"], t - 1)
                for half in range(2):
                    for c in range(CH):
                        last = mm(bank[2 * (t % 2) + half][:, :], hnT[:, c, t * P:(t + 1) * P],
                                  g_sb[:, c, t // TPB, 4 * half:4 * half + 4, :].rearrange("p a b -> p (a b)"),
                                  start=(c == 0), stop=(c == CH - 1))
                last.then_inc(S["scores"], 1)

            pe.wait_ge(S["ld_const"], 16)
            seen = set()
            for n, (kind, j) in enumerate(items):
                b = bank[bank_of[n]]
                if n == NV:
                    settle(NV - 1)
                    scores(0)
                if n == NV + 4:
                    scores(1)
                if n >= 8:
                    settle(n - 8 if n < NV + 4 else n - 4)
                first = kind not in seen
                seen.add(kind)
                if kind == "K":
                    pe.wait_ge(S["ctx_roped"], 1)
                    for c in range(2):
                        last = tr(b[:, c * P:(c + 1) * P], kvr[:, c, :], ident)
                if kind == "A":
                    pe.wait_ge(S[f"ld_wqr{j}"], 16)
                    pe.wait_ge(S[f"ld_wkcq{j}"], 16)
                    for q in range(4):
                        for c in range(QC):
                            for h2 in range(2):
                                h = 8 * j + 2 * q + h2
                                last = mm(b[h2 * RK:(h2 + 1) * RK, q * HK:(q + 1) * HK], wqr[0:QP, h, c, :],
                                          wkcq[0:QP, h, c, :], start=(c == 0), stop=(c == QC - 1))
                if kind == "E":
                    if first:
                        pe.wait_ge(S["ld_wkr"], 16)
                        settle(last_of("A"))
                    for p in range(PAIRS):
                        rs = slice(j * RK, (j + 1) * RK)
                        last = mm(b[:, p * DC:(p + 1) * DC], a_sb[rs, p, :], wkr[rs, p, :], start=True, stop=True)
                if kind == "C":
                    if first:
                        pe.wait_ge(S["ld_wq"], 16)
                        settle(last_of("E"))
                    for q in range(2):
                        for h2 in range(2):
                            h = 4 * j + 2 * q + h2
                            last = mm(b[h2 * DC:(h2 + 1) * DC, q * DIM:(q + 1) * DIM], e_sb[:, h, :], wq[:, h, :],
                                      start=True, stop=True)
                if kind == "F":
                    if first:
                        pe.wait_ge(S["ld_wkv"], 16)
                        pe.wait_ge(S["ld_wo"], 16)
                    for q in range(2):
                        for h2 in range(2):
                            h = 4 * j + 2 * q + h2
                            last = mm(b[h2 * DC:(h2 + 1) * DC, q * DIM:(q + 1) * DIM], wkv[:, h, :], wo[:, h, :],
                                      start=True, stop=True)
                if kind == "H":
                    pe.wait_ge(S["hn1"], 2 * j + 2)
                    for q in range(2):
                        for c in range(CH):
                            o = (c * 2 + q) * P
                            last = tr(b[:, o:o + P], hn[:, 2 * j + q, c * P:(c + 1) * P], ident)
                if kind == "G":
                    if first:
                        settle(last_of("C"))
                    p, c = j // 2, j % 2
                    last = mm(b[:, :], c_sb[:, p, c * P:(c + 1) * P],
                              bd[:, :, :, :].rearrange("p b h k -> p (b h k)"), start=True, stop=True)
                if kind == "V":
                    p, bp = j // 2, j % 2
                    for q in range(2):
                        last = mm(b[:, q * DIM:(q + 1) * DIM],
                                  bd[:, 2 * bp + q, :, :].rearrange("p h k -> p (h k)"),
                                  f_sb[:, p, :], start=True, stop=True)
                last.then_inc(S["prep_mm"], 1)

            settle(NI - 1)

            def turn_probs(t):
                pe.wait_ge(S["probs"], t + 1)
                if t:
                    pe.wait_ge(S["pt_sb"], 2 * t)
                for half in range(2):
                    for q in range(4):
                        p = 4 * half + q
                        last = tr(bank[4 + half][:, q * P:(q + 1) * P], p_sb[:, t % 2, p * P:(p + 1) * P], ident)
                    last.then_inc(S["pt"], 1)

            def attend(t):
                if t:
                    pe.wait_ge(S["x_ok"], t)
                for p in range(PAIRS):
                    if p % 4 == 0:
                        pe.wait_ge(S["pt_sb"], 2 * t + 1 + p // 4)
                    last = mm(bank[6][:, 0:DIM], pt_sb[:, t % 2, p, :], v_sb[:, t // TPB, p, :],
                              start=(p == 0), stop=(p == PAIRS - 1))
                last.then_inc(S["attn"], 1)

            turned, chunks_asked, slots_asked = [0], [0], [0]

            def bank7_read():
                if turned[0]:
                    pe.wait_ge(S["hn2T_sb"], turned[0])
                if chunks_asked[0]:
                    pe.wait_ge(S["elog"], chunks_asked[0])
                if slots_asked[0]:
                    pe.wait_ge(S["slot_read"], slots_asked[0])

            def turn_hn2(t):
                pe.wait_ge(S["hn2"], t + 1)
                bank7_read()
                for c in range(CH):
                    last = tr(bank[7][:, c * P:(c + 1) * P], hn[:, t, c * P:(c + 1) * P], ident)
                last.then_inc(S["hn2T"], 1)
                turned[0] = t + 1

            def route_logits(t):
                bank7_read()
                if t == 0:
                    pe.wait_ge(S["ld_router"], 32)
                o = 256 + (t - max(f for f, _ in CHUNKS if f <= t)) * EXP
                for c in range(CH):
                    last = mm(bank[7][:, o:o + EXP], hnT[:, c, t * P:(t + 1) * P], rw[:, c, :],
                              start=(c == 0), stop=(c == CH - 1))
                last.then_inc(S["logits"], 1)
                chunks_asked[0] = sum(first + n <= t + 1 for first, n in CHUNKS)

            def slot_numbers(k):
                pe.wait_ge(S["pick"], k + 1)
                if k:
                    pe.wait_ge(S["base"], k)
                bank7_read()
                first, n = CHUNKS[k]
                for r in range(n):
                    o = 384 + r * EXP
                    mm(bank[7][:, o:o + EXP], tri16[:, :], pick16[:, first + r, :], start=True, stop=False)
                    for q in range(r):
                        mm(bank[7][:, o:o + EXP], ones16[:, :], pick16[:, first + q, :], start=False, stop=False)
                    last = mm(bank[7][:, o:o + EXP], ones16[:, :], base16[:, k, :], start=False, stop=True)
                last.then_inc(S["slotnum"], 1)
                slots_asked[0] = k + 1

            def shared_gate_up(half):
                if half == 0:
                    pe.wait_ge(S["ld_sh"], 32)
                    pe.wait_ge(S["expd"], TILES)
                pe.wait_ge(S["hn2T_sb"], 4 * half + 4)
                for gu in range(2):
                    for c in range(CH):
                        last = mm(bank[2 * half + gu][0:FF, :], shw[:, gu * CH + c, :],
                                  hnT[:, c, half * 512:(half + 1) * 512], start=(c == 0), stop=(c == CH - 1))
                last.then_inc(S["sh_gu"], 1)

            for t in range(TILES + 2):
                if t < TILES:
                    turn_probs(t)
                if t >= 2:
                    route_logits(t - 2)
                if t >= TILES:
                    shared_gate_up(t - TILES)
                if t in PE_SLOTS:
                    slot_numbers(PE_SLOTS[t])
                if t + 2 < TILES:
                    scores(t + 2)
                if t < TILES:
                    attend(t)
                if 1 <= t <= TILES:
                    turn_hn2(t - 1)
            for k in range(slots_asked[0], NC):
                slot_numbers(k)
            for t in range(TILES):
                if t % 4 == 0:
                    pe.wait_ge(S["sh_h"], t // 4 + 1)
                if t == 0:
                    pe.wait_ge(S["pt_sb"], 2 * TILES)
                b = bank[(4, 5, 2, 3)[t // 2]]
                last = mm(b[:, (t % 2) * DIM:(t % 2 + 1) * DIM], h_sh[0:FF, t * P:(t + 1) * P], shd[0:FF, :],
                          start=True, stop=True)
                if t % 2:
                    last.then_inc(S["sh_dn"], 1)

            def turn_rows(n):
                i, pr = n // 4, n % 4
                if pr % 2 == 0:
                    pe.wait_ge(s_xe[i % XS][pr // 2], 16 * (i // XS + 1))
                if n >= 2:
                    pe.wait_ge(S["xt_ok"], n - 1)
                for q in range(2):
                    for c in range(CH):
                        last = tr(bank[n % 2][:, (q * CH + c) * P:(q * CH + c + 1) * P],
                                  xe[i % XS][:, 2 * pr + q, c * P:(c + 1) * P], ident)
                last.then_inc(S["tx"], 1)

            def gate_up(n):
                i, pr = n // 4, n % 4
                if pr == 0:
                    pe.wait_ge(s_w[i % WSLOTS], 32 * (i // WSLOTS + 1))
                pe.wait_ge(S["xt_ok"], n + 1)
                if n >= 2:
                    pe.wait_ge(S["h"], n - 1)
                for q in range(2):
                    for c in range(CH):
                        last = mm(bank[2 + n % 2][:, q * 2 * FF:(q + 1) * 2 * FF], xt[n % 2][:, q, c, :],
                                  wgu_sb[i % WSLOTS][:, 2 * pr + q, c, :], start=(c == 0), stop=(c == CH - 1))
                last.then_inc(S["gu"], 1)

            def turn_hidden(n):
                pe.wait_ge(S["h"], n + 1)
                if n >= 2:
                    pe.wait_ge(S["ht_ok"], n - 1)
                for q in range(2):
                    last = tr(bank[4 + n % 2][0:FF, q * CAP:(q + 1) * CAP], hw[n % 2][:, q, :], ident)
                last.then_inc(S["th"], 1)

            def down(n):
                i, pr = n // 4, n % 4
                pe.wait_ge(S["ht_ok"], n + 1)
                if n >= 2:
                    pe.wait_ge(S["y_ok"], n - 1)
                for q in range(2):
                    last = mm(bank[6 + n % 2][:, q * DIM:(q + 1) * DIM], ht[n % 2][0:FF, q, :],
                              wdn_sb[i % WSLOTS][0:FF, 2 * pr + q, :], start=True, stop=True)
                last.then_inc(S["dn"], 1)

            pe.wait_ge(S["sh_added"], TILES // 2)
            pe.wait_ge(S["slot_read"], NC)
            NP = EXP // 2
            for n in range(NP + 3):
                if n < NP:
                    turn_rows(n)
                if 2 <= n < NP + 2:
                    turn_hidden(n - 2)
                if 1 <= n < NP + 1:
                    gate_up(n - 1)
                if n >= 3:
                    down(n - 3)

        @block.scalar
        def _(act):
            A = nc.scalar.activation
            nc.scalar.preload_act_table_set("natural_log_exp_and_others")

            def copy_out(o, i):
                return A(o, i, ACT.Copy)

            def rsqrt_seed(ts, ready, n, done):
                act.wait_ge(ready, n)
                A(lnv[:, ts], veps[:, ts], ACT.Ln).then_inc(S["a_chain"], 1)
                act.wait_ge(S["a_chain"], n)
                A(rs0[:, ts], lnv[:, ts], ACT.Exp, scale=-0.5).then_inc(done, 1)

            def exp_scores(t, h0=0, h1=HEADS):
                if h0 == 0:
                    act.wait_ge(S["nmax"], t + 1)
                    if t >= 2:
                        act.wait_ge(S["pt"], 2 * (t - 1))
                for h in range(h0, h1):
                    last = A(p_sb[:, t % 2, h * KEYS:(h + 1) * KEYS],
                             bank[2 * (t % 2) + h // 8][:, h % 8 * KEYS:(h % 8 + 1) * KEYS], ACT.Exp,
                             bias=rmax[:, t % 2, h:h + 1], accum_out=rsum[:, t % 2, h:h + 1])
                if h1 == HEADS:
                    last.then_inc(S["expd"], 1)

            for n, (kind, j) in enumerate(items):
                if n == 3:
                    rsqrt_seed(slice(0, TILES), S["stats1"], 1, S["rstd1"])
                if by_act[n]:
                    act.wait_ge(S["prep_mm"], n + 1)
                    move_out(act, kind, j, n, copy_out, S["prep_act"])
                if NV + 3 <= n < NV + TPV and by_act[n]:
                    q = (n - NV) // 3 - 1
                    exp_scores(0, 4 * q, 4 * q + 4) if q < 4 else None
            exp_scores(1)

            for t in range(TILES + 2):
                if t < TILES:
                    for half in range(2):
                        act.wait_ge(S["pt"], 2 * t + half + 1)
                        if t >= 2:
                            act.wait_ge(S["attn"], t - 1)
                        A(pt_sb[:, t % 2, 4 * half:4 * half + 4, :],
                          bank[4 + half][:, :].rearrange("p (a b) -> p a b", b=P), ACT.Copy).then_inc(S["pt_sb"], 1)
                k = [k for k, (first, n) in enumerate(CHUNKS) if first + n == t - 1]
                if k:
                    n = CHUNKS[k[0]][1]
                    act.wait_ge(S["logits"], t - 1)
                    if k[0]:
                        act.wait_ge(S["pick"], k[0])
                    A(el[:, 0:n, :], bank[7][:, 256:256 + n * EXP].rearrange("p (r e) -> p r e", r=n), ACT.Exp,
                      scale=-1.0).then_inc(S["elog"], 1)
                if 1 <= t <= TILES:
                    act.wait_ge(S["stats2"], t)
                    A(lnv[:, t - 1:t], veps[:, t - 1:t], ACT.Ln).then_inc(S["a_chain"], 1)
                    act.wait_ge(S["a_chain"], t + 1)
                    A(rs0[:, t - 1:t], lnv[:, t - 1:t], ACT.Exp, scale=-0.5).then_inc(S["rstd2"], 1)
                if t + 2 < TILES:
                    exp_scores(t + 2)
                if 1 <= t <= TILES:
                    act.wait_ge(S["hn2T"], t)
                    act.wait_ge(S["scores"], t)
                    A(hnT[:, :, (t - 1) * P:t * P], bank[7][:, 0:DIM].rearrange("p (c q) -> p c q", c=CH),
                      ACT.Copy).then_inc(S["hn2T_sb"], 1)
            for half in range(2):
                act.wait_ge(S["sh_gu"], half + 1)
                if half:
                    act.wait_ge(S["sh_h"], half)
                A(sg_sh[0:FF, :], bank[2 * half][0:FF, :], ACT.Silu).then_inc(S["sh_act"], 1)

            def rows_out(n):
                act.wait_ge(S["tx"], n + 1)
                if n >= 2:
                    act.wait_ge(S["gu"], n - 1)
                A(xt[n % 2], bank[n % 2][:, :].rearrange("p (q c s) -> p q c s", q=2, c=CH),
                  ACT.Copy).then_inc(S["xt_ok"], 1)

            def hidden_out(n):
                act.wait_ge(S["th"], n + 1)
                if n >= 2:
                    act.wait_ge(S["dn"], n - 1)
                A(ht[n % 2][0:FF], bank[4 + n % 2][0:FF, 0:2 * CAP].rearrange("p (q s) -> p q s", q=2),
                  ACT.Copy).then_inc(S["ht_ok"], 1)

            def silu(n):
                act.wait_ge(S["gu"], n + 1)
                if n >= 2:
                    act.wait_ge(S["h"], n - 1)
                A(sg[n % 2], bank[2 + n % 2][:, 0:4 * FF].rearrange("p (q u f) -> p q u f", q=2, u=2)[:, :, 0, :],
                  ACT.Silu).then_inc(S["silu"], 1)
            NP = EXP // 2
            for n in range(NP + 2):
                if n < NP:
                    rows_out(n)
                if n >= 2:
                    hidden_out(n - 2)
                if 1 <= n < NP + 1:
                    silu(n - 1)

        @block.vector
        def _(dve):
            V = nc.vector
            n_chain = [0]

            def then(ins):
                n_chain[0] += 1
                ins.then_inc(S["d_chain"], 1)
                dve.wait_ge(S["d_chain"], n_chain[0])

            V.memset(bd[:, :, :, :], 0.0).then_inc(S["bd_zero"], 1)
            V.memset(zeros, 0.0).then_inc(S["zero_ok"], 1)
            V.memset(base16[:, 0, :], 0.0)
            V.memset(ones16[:, :], 1.0)
            V.memset(hn[:, :, C_NUM:ROW], 0.0)
            then(V.memset(gpad, BIG))
            dve.wait_ge(S["ld_ctx"], 16)
            dve.wait_ge(S["ld_const"], 16)
            V.tensor_copy(tri16[:, :], const[:, C_TRI:C_TRI + P])
            V.tensor_copy(hn[:, :, C_NUM].bitcast(u32), const[:, C_TOK:C_TOK + TILES])
            cosv, sinv = const[:, C_COS:C_COS + DC], const[:, C_SIN:C_SIN + DC]
            hd = DC // 2
            for c in range(2):
                V.tensor_tensor(kvt[:, c, 0:hd], ctx_sb[:, c, hd:DC], sinv[:, 0:hd], ALU.mult)
                V.tensor_tensor(kvt[:, c, hd:DC], ctx_sb[:, c, 0:hd], sinv[:, hd:DC], ALU.mult)
                then(V.tensor_tensor(kvr[:, c, 0:DC], ctx_sb[:, c, :], cosv, ALU.mult))
                then(V.tensor_tensor(kvr[:, c, 0:DC], kvr[:, c, 0:DC], kvt[:, c, :], ALU.add))
                last = V.tensor_copy(kvr[:, c, DC:2 * DC], kvr[:, c, 0:DC])
            last.then_inc(S["ctx_roped"], 1)

            def ln_stats(t):
                then(V.bn_stats(stats[:, t, :], x[:, t, :]))
                return V.bn_aggr(mv[:, t, :], stats[:, t, :])

            def refine(ts, y2):
                then(V.tensor_tensor(rs1[:, ts], y2, veps[:, ts], ALU.mult))
                then(V.tensor_scalar(rs1[:, ts], rs1[:, ts], -0.5, 1.5, ALU.mult, ALU.add))
                then(V.tensor_tensor(rstd[:, ts], rs0[:, ts], rs1[:, ts], ALU.mult))

            dve.wait_ge(S["ld_x"], 16)
            for t in range(TILES):
                last = ln_stats(t)
            then(last)
            V.tensor_scalar_add(veps, mv[:, :, 1], EPS).then_inc(S["stats1"], 1)
            dve.wait_ge(S["rstd1"], 1)
            then(V.tensor_tensor(rstd, rs0, rs0, ALU.mult))
            refine(slice(0, TILES), rstd)
            for t in range(TILES):
                V.tensor_scalar(hn[:, t, 0:DIM], x[:, t, :], mv[:, t, 0:1], rstd[:, t:t + 1],
                                ALU.subtract, ALU.mult).then_inc(S["hn1"], 1)

            def soften(t):
                dve.wait_ge(S["scores"], t + 1)
                if t >= 2:
                    dve.wait_ge(S["expd"], t - 1)
                for half in range(2):
                    last = V.tensor_reduce(rmax[:, t % 2, 8 * half:8 * half + 8],
                                           bank[2 * (t % 2) + half][:, :].rearrange("p (h k) -> p h k", h=8),
                                           AX.X, ALU.max, negate=True)
                last.then_inc(S["nmax"], 1)

            for n, (kind, j) in enumerate(items):
                if not by_act[n]:
                    dve.wait_ge(S["prep_mm"], n + 1)
                    move_out(dve, kind, j, n, V.tensor_copy, S["prep_dve"])
                if n == NV:
                    soften(0)
                if n == NV + 4:
                    soften(1)

            def normalise(t):
                dve.wait_ge(S["expd"], t + 1)
                then(V.reciprocal(rsum[:, t % 2, :], rsum[:, t % 2, :]))
                v = p_sb[:, t % 2, :].rearrange("p (h k) -> p h k", h=HEADS)
                V.tensor_tensor(v, v, rsum[:, t % 2, :].unsqueeze(2).to_broadcast([P, HEADS, KEYS]),
                                ALU.mult).then_inc(S["probs"], 1)

            def add_attn(t):
                dve.wait_ge(S["attn"], t + 1)
                V.tensor_tensor(x[:, t, :], x[:, t, :], bank[6][:, 0:DIM], ALU.add).then_inc(S["x_ok"], 1)
                dve.wait_ge(S["x_ok"], t + 1)
                then(ln_stats(t))
                V.tensor_scalar_add(veps[:, t:t + 1], mv[:, t, 1:2], EPS).then_inc(S["stats2"], 1)

            def second_norm(t):
                dve.wait_ge(S["rstd2"], t + 1)
                ts = slice(t, t + 1)
                then(V.tensor_tensor(rstd[:, ts], rs0[:, ts], rs0[:, ts], ALU.mult))
                refine(ts, rstd[:, ts])
                V.tensor_scalar(hn[:, t, 0:DIM], x[:, t, :], mv[:, t, 0:1], rstd[:, t:t + 1],
                                ALU.subtract, ALU.mult).then_inc(S["hn2"], 1)

            def pick_experts(k):
                first, n = CHUNKS[k]
                dve.wait_ge(S["elog"], k + 1)
                R = slice(0, n)
                then(V.tensor_scalar_add(s0[:, R], el[:, R], 1.0))
                then(V.reciprocal(s0[:, R], s0[:, R]))
                then(V.tensor_tensor(sc[:, R], s0[:, R], ebias.unsqueeze(1).to_broadcast([P, n, EXP]), ALU.add))
                g = sc[:, R].rearrange("p r (g e) -> p r g e", g=GRP)
                V.tensor_tensor(m1[:, R], g[:, :, :, 0:4], g[:, :, :, 4:8], ALU.max)
                then(V.tensor_tensor(n1[:, R], g[:, :, :, 0:4], g[:, :, :, 4:8], ALU.min))
                V.tensor_tensor(m2[:, R], m1[:, R, :, 0:2], m1[:, R, :, 2:4], ALU.max)
                V.tensor_tensor(t2[:, R], m1[:, R, :, 0:2], m1[:, R, :, 2:4], ALU.min)
                then(V.tensor_tensor(n2[:, R], n1[:, R, :, 0:2], n1[:, R, :, 2:4], ALU.max))
                then(V.tensor_tensor(n2[:, R], n2[:, R], t2[:, R], ALU.max))
                V.tensor_tensor(gs[:, R], m2[:, R, :, 0], m2[:, R, :, 1], ALU.max)
                V.tensor_tensor(t3[:, R], m2[:, R, :, 0], m2[:, R, :, 1], ALU.min)
                then(V.tensor_tensor(n3[:, R], n2[:, R, :, 0], n2[:, R, :, 1], ALU.max))
                then(V.tensor_tensor(n3[:, R], n3[:, R], t3[:, R], ALU.max))
                then(V.tensor_tensor(gpad[:, R, 0:GRP], gs[:, R], n3[:, R], ALU.add))
                for r in range(n):
                    ins = V.max(top4[:, r, :], gpad[:, r, 0:GRP])
                then(ins)
                then(V.memset(top4[:, R, TOPG:8], BIG))
                for r in range(n):
                    ins = V.match_replace(rep[:, r, 0:16], top4[:, r, :], gpad[:, r, :], -BIG)
                then(ins)
                then(V.tensor_single_scalar(gpick[:, R], rep[:, R, 0:GRP], -BIG, ALU.is_equal))
                then(V.tensor_tensor(msk[:, R].rearrange("p r (g e) -> p r g e", g=GRP), g,
                                     gpick[:, R].unsqueeze(3).to_broadcast([P, n, GRP, EPG]), ALU.mult))
                for r in range(n):
                    ins = V.max(top8[:, r, :], msk[:, r, :])
                then(ins)
                for r in range(n):
                    ins = V.match_replace(rep[:, r, :], top8[:, r, :], msk[:, r, :], -BIG)
                then(ins)
                V.tensor_single_scalar(pick16[:, first:first + n, :], rep[:, R], -BIG, ALU.is_equal).then_inc(S["pick"], 1)
                dve.wait_ge(S["pick"], k + 1)
                if k + 1 < NC:
                    prev = base16[:, k, :]
                    for r in range(n):
                        ins = V.tensor_tensor(base16[:, k + 1, :], prev, pick16[:, first + r, :], ALU.add)
                        prev = base16[:, k + 1, :]
                        if r + 1 < n:
                            then(ins)
                    ins.then_inc(S["base"], 1)
                for r in range(n):
                    t = first + r
                    ins = V.scalar_tensor_tensor(s0[:, r, :], s0[:, r, :], 1.0, pick16[:, t, :], ALU.mult, ALU.mult,
                                                 accum_out=wsum[:, t:t + 1])
                then(ins)
                then(V.tensor_scalar_add(wsum[:, first:first + n], wsum[:, first:first + n], 1e-20))
                then(V.reciprocal(wsum[:, first:first + n], wsum[:, first:first + n]))
                for r in range(n):
                    t = first + r
                    V.tensor_scalar(hn[:, t, DIM:DIM + EXP], s0[:, r, :], wsum[:, t:t + 1], SCALE,
                                    ALU.mult, ALU.mult).then_inc(S["weights"], 1)

            def place_experts(k):
                first, n = CHUNKS[k]
                R = slice(0, n)
                dve.wait_ge(S["slotnum"], k + 1)
                V.scalar_tensor_tensor(slot[:, R], pick16[:, first:first + n, :], -UNPICKED,
                                       bank[7][:, 384:384 + n * EXP].rearrange("p (r e) -> p r e", r=n),
                                       ALU.mult, ALU.add).then_inc(S["slot_read"], 1)
                dve.wait_ge(S["slot_read"], k + 1)
                then(V.scalar_tensor_tensor(key1[:, R], slot[:, R], float(GRP),
                                            const[:, C_KEY:C_KEY + EXP].unsqueeze(1).to_broadcast([P, n, EXP]),
                                            ALU.mult, ALU.add))
                then(V.scalar_tensor_tensor(keys[:, R], slot[:, R], FAR, key1[:, R], ALU.is_lt, ALU.mult))
                for r in range(n):
                    ins = V.max(key8[:, r, :], keys[:, r, :])
                then(ins)
                then(V.tensor_scalar(over[:, R], key8[:, R], 0.0, const[:, C_DUMP:C_DUMP + 1], ALU.is_equal, ALU.mult))
                V.scalar_tensor_tensor(rows8[:, first * TOPK:(first + n) * TOPK].rearrange("p (r k) -> p r k", r=n),
                                       key8[:, R], -1.0, over[:, R], ALU.add, ALU.add).then_inc(S["rows"], 1)

            normalise(0)
            for t in range(TILES + 3):
                if 1 <= t <= TILES:
                    add_attn(t - 1)
                if t + 1 < TILES:
                    normalise(t + 1)
                if 1 <= t <= TILES:
                    second_norm(t - 1)
                if t + 2 < TILES:
                    soften(t + 2)
                if t in PE_SLOTS:
                    place_experts(PE_SLOTS[t])
                if t in DVE_PICKS:
                    pick_experts(DVE_PICKS[t])

            for half in range(2):
                dve.wait_ge(S["sh_act"], half + 1)
                V.tensor_tensor(h_sh[0:FF, half * 512:(half + 1) * 512], sg_sh[0:FF, :], bank[2 * half + 1][0:FF, :],
                                ALU.mult).then_inc(S["sh_h"], 1)
            for j in range(TILES // 2):
                dve.wait_ge(S["sh_dn"], j + 1)
                b = bank[(4, 5, 2, 3)[j]]
                V.tensor_tensor(x[:, 2 * j:2 * j + 2, :], x[:, 2 * j:2 * j + 2, :],
                                b[:, :].rearrange("p (t m) -> p t m", t=2), ALU.add).then_inc(S["sh_added"], 1)

            def hidden(n):
                i, pr = n // 4, n % 4
                dve.wait_ge(S["silu"], n + 1)
                if n >= 2:
                    dve.wait_ge(S["th"], n - 1)
                for q in range(2):
                    g = 2 * pr + q
                    last = V.scalar_tensor_tensor(
                        hw[n % 2][:, q, :], sg[n % 2][:, q, :],
                        xe[i % XS][:, g, DIM + GRP * g + i:DIM + GRP * g + i + 1],
                        bank[2 + n % 2][:, (2 * q + 1) * FF:(2 * q + 2) * FF], ALU.mult, ALU.mult)
                last.then_inc(S["h"], 1)

            def y_out(n):
                dve.wait_ge(S["dn"], n + 1)
                for s in range(NSUM):
                    if sums_after(2 * (n - YS + 1), s) > 0:
                        dve.wait_ge(s_sum[s], sums_after(2 * (n - YS + 1), s))
                V.tensor_copy(ysb[n % YS], bank[6 + n % 2][:, :].rearrange("p (q m) -> p q m", q=2)
                              ).then_inc(S["y_ok"], 1)
            NP = EXP // 2
            for n in range(1, NP + 3):
                if n < NP + 1:
                    hidden(n - 1)
                if n >= 3:
                    y_out(n - 3)
            for hf in range(2):
                ts = slice(hf * TILES // 2, (hf + 1) * TILES // 2)
                for s in range(NSUM):
                    dve.wait_ge(s_acc[s][hf], 16)
                    if s:
                        dve.wait_ge(S["added"], NSUM * hf + s)
                    V.tensor_tensor(x[:, ts, :], x[:, ts, :], acc[s][:, ts, :], ALU.add).then_inc(S["added"], 1)

        @block.gpsimd
        def _(pool):
            G = nc.gpsimd
            pool.wait_ge(S["filled"], 16 * EPG)
            t = 0
            for k, (first, n) in enumerate(CHUNKS):
                pool.wait_ge(S["rows"], k + 1)
                pool.wait_ge(S["weights"], first + n)
                for m in range(first * TOPK, (first + n) * TOPK):
                    G.indirect_dma_start(
                        out=xe_table[:, :], out_offset=bass.IndirectOffsetOnAxis(ap=rows8[:, m:m + 1], axis=0),
                        in_=hn[:, m // TOPK, :], in_offset=None,
                        bounds_check=EXP * CAP - 1, oob_is_err=False).then_inc(S["spread"], 16)
            pool.wait_ge(S["zeroed"], 16 * NSUM)
            for n in range(EXP // 2):
                i, pr = n // 4, n % 4
                pool.wait_ge(S["y_ok"], n + 1)
                for q in range(2):
                    m = 2 * n + q
                    s = m % NSUM
                    if m >= NSUM:
                        pool.wait_ge(s_sum[s], 16 * (m // NSUM))
                    G.indirect_dma_start(
                        out=sums[s][:, :],
                        out_offset=bass.IndirectOffsetOnAxis(
                            ap=xe[i % XS][:, 2 * pr + q, C_NUM:C_NUM + 1].bitcast(u32), axis=0),
                        in_=ysb[n % YS][:, q, :], in_offset=None, compute_op=ALU.add).then_inc(s_sum[s], 16)


def constants():
    import numpy as np
    c = np.zeros((P, C_ALL), np.float32)
    c[:, C_IDENT:C_IDENT + P] = np.eye(P)
    e = np.arange(EXP)
    c[:, C_KEY:C_KEY + EXP] = (e % EPG) * GRP * CAP + e // EPG + 1 + GRP * UNPICKED
    c[:, C_DUMP] = EXP * CAP + 1 + np.arange(P)
    c[:, C_TOK:C_TOK + TILES] = np.arange(P)[:, None] + P * np.arange(TILES)
    inv = (1.0 / np.float32(10000.0) ** (np.arange(0, DC, 2, dtype=np.float32) / np.float32(DC))).astype(np.float32)
    fr = np.arange(KEYS, dtype=np.float32)[:, None] * inv[None, :]
    cos, sin = np.repeat(np.cos(fr), 2, -1), np.repeat(np.sin(fr), 2, -1)
    sin[:, :DC // 2] *= -1.0
    c[:, C_COS:C_COS + DC] = np.tile(cos, (P // KEYS, 1))
    c[:, C_SIN:C_SIN + DC] = np.tile(sin, (P // KEYS, 1))
    c[:, C_TRI:C_TRI + P] = np.triu(np.ones((P, P)), 1)
    return c


def empty_row():
    import numpy as np
    r = np.zeros((P, ROW), np.float32)
    r[:, C_NUM] = (TOK + np.arange(P)).astype(np.uint32).view(np.float32)
    return r


def kernel(**inputs):
    import numpy as np
    import concourse.bacc as bacc
    from concourse.bass_utils import run_bass_kernel_spmd

    v = {k.removeprefix("L0_"): np.asarray(a) for k, a in inputs.items()}

    def pack(w):
        e, r, c = w.shape
        return w.reshape(GRP, EPG, r // P, P, c).transpose(1, 3, 0, 2, 4)
    gate, up = pack(v["ffn_w_gate"]), pack(v["ffn_w_up"])
    d = {
        "x": v["x"].reshape(TOK, DIM),
        "ctx": v["ctx_512"].reshape(2, P, DC).transpose(1, 0, 2),
        "const": constants(),
        "empty": empty_row(),
        "wq": v["xattn_Wq"].reshape(HEADS, HK, DIM).transpose(1, 0, 2),
        "wkcq": v["xattn_w_kc_q"].reshape(HEADS, HK, QC, QP).transpose(3, 0, 2, 1),
        "wqr": v["xattn_W_qr"].reshape(HEADS, QC, QP, RK).transpose(2, 0, 1, 3),
        "wkr": v["xattn_W_kr"].reshape(PAIRS, 2, DC, RK).transpose(1, 3, 0, 2).reshape(2 * RK, PAIRS, DC),
        "wkv": v["xattn_w_kc_kv"].transpose(1, 0, 2),
        "wo": v["xattn_Wo"].reshape(DIM, HEADS, HK).transpose(2, 1, 0),
        "rw": v["ffn_router_weight"].reshape(EXP, CH, P).transpose(2, 1, 0),
        "ebias": np.tile(v["ffn_e_bias"].reshape(1, EXP), (P, 1)),
        "shw": np.concatenate([v[n].reshape(CH, P, FF).transpose(1, 0, 2) for n in ("ffn_sh_gate", "ffn_sh_up")], 1),
        "shd": v["ffn_sh_down"],
        "wgu": np.concatenate([gate, up], 4).reshape(EPG, P, GRP * 2 * CH * FF),
        "wdn": v["ffn_w_down"].reshape(GRP, EPG, FF, DIM).transpose(1, 2, 0, 3).reshape(EPG, FF, GRP * DIM),
    }
    nc = bacc.Bacc("TRN2", target_bir_lowering=False, num_devices=1)
    arrays, aps = {}, {}
    for name, arr in d.items():
        arr = np.ascontiguousarray(arr)
        arrays[f"in_{name}"] = arr
        aps[name] = nc.dram_tensor(f"in_{name}", arr.shape, mybir.dt.float32, kind="ExternalInput").ap()
    out = nc.dram_tensor("out", (TOK, DIM), mybir.dt.float32, kind="ExternalOutput").ap()
    program(nc, aps, out, None)
    r = run_bass_kernel_spmd(nc, [arrays], core_ids=[0])
    return r.results[0]["out"].reshape(BATCH, SEQ, DIM)
```

```python
import concourse.bass as bass
from concourse import mybir
from contextlib import ExitStack

P = 128
BATCH, SEQ, DIM = 4, 256, 256
TOK = BATCH * SEQ
TILES = TOK // P
TPB = SEQ // P
KEYS, DC = 64, 64
HEADS, HK, DQ, RK = 16, 128, 192, 64
PAIRS = HEADS // 2
QC = 2
QP = DQ // QC
CH = DIM // P
EXP, GRP, EPG = 64, 8, 8
TOPG, TOPK, FF = 4, 8, 88
CAP = 128
SCALE = 2.5
EPS = 1e-5
OUTS = 4
NSUM = 4
TABLE = [m % 4 if m < 48 else m % 3 if m < 60 else m % 2 for m in range(EXP)]
CLOSING = (3, 2, 0, 1)
BIG = 3.0e38
PICKED = 2048.0
FAR = CAP - PICKED
NOROW = 2.0 * EXP * CAP
ROW = DIM + EXP + 4
C_NUM = DIM + EXP

C_IDENT = 0
C_KEY = C_IDENT + P
C_TOK = C_KEY + EXP
C_COS = C_TOK + TILES
C_SIN = C_COS + DC
C_TRI = C_SIN + DC
C_ALL = C_TRI + P


def program(nc, a, out):
    f32, f16, u32 = mybir.dt.float32, mybir.dt.float16, mybir.dt.uint32
    ALU, ACT, AX = mybir.AluOpType, mybir.ActivationFunctionType, mybir.AxisListType
    ctx = ExitStack()
    with ctx:
        def sb(name, shape, dt=f32):
            return ctx.enter_context(nc.sbuf_tensor(name, shape, dt))

        def sem(name):
            return ctx.enter_context(nc.semaphore(name))

        xe_table = nc.dram_tensor("xe_table", (EXP * CAP, ROW), f32, kind="Internal").ap()
        sums = [nc.dram_tensor(f"sums{s}", (TOK + CAP, DIM), f32, kind="Internal").ap() for s in range(NSUM)]

        const = sb("const", [P, C_ALL])
        x = sb("x", [P, TILES, DIM])
        hn = sb("hn", [P, TILES, ROW])
        hnT = sb("hnT", [P, CH, TOK])
        bd = sb("bd", [P, BATCH, 2, KEYS])
        g_sb = sb("g_sb", [P, CH, BATCH, PAIRS, P])
        v_sb = sb("v_sb", [P, BATCH, PAIRS, DIM])
        region = sb("region", [P, 26624])
        small = sb("small", [P, 2048])
        near16 = sb("near16", [P, P], f16)
        ones16 = sb("ones16", [P, P], f16)

        def view(base, off, *dims):
            n = 1
            for d in dims:
                n *= d
            ap = base[:, off:off + n]
            if len(dims) == 2:
                ap = ap.rearrange("p (a b) -> p a b", b=dims[1])
            if len(dims) == 3:
                ap = ap.rearrange("p (a b c) -> p a b c", b=dims[1], c=dims[2])
            if len(dims) == 4:
                ap = ap.rearrange("p (a b c d) -> p a b c d", b=dims[1], c=dims[2], d=dims[3])
            return ap

        wkcq = view(region, 0, HEADS, QC, HK)
        wqr = view(region, 4096, HEADS, QC, RK)
        wkr = view(region, 6144, PAIRS, 2, DC)
        a_sb = view(region, 8192, PAIRS, HK)
        e_sb = view(region, 10240, HEADS, DC)
        wkv = view(region, 11264, HEADS, DC)
        wq = view(region, 12288, HEADS, DIM)
        wo = view(region, 16384, HEADS, DIM)
        c_sb = view(region, 20480, PAIRS, DIM)
        f_sb = view(region, 22528, PAIRS, DIM)
        ctx_sb = view(region, 24576, 2, DC)
        kvr = view(region, 24704, 2, 2 * DC)
        kvt = view(region, 24960, 2, DC)
        p_sb = view(region, 4864, 2, HEADS * KEYS)
        pt_sb = view(region, 6912, 2, PAIRS, P)
        WG = EPG * CH * 2 * FF
        WD = EPG * DIM
        WSLOTS = 4
        w_at = [12288, 12288 + WG + WD, 0, WG + WD]
        wgu_sb = [view(region, o, EPG, CH, 2 * FF) for o in w_at]
        wdn_sb = [view(region, o + WG, EPG, DIM) for o in w_at]
        h_sh = view(region, 22016, TOK)
        empty = view(region, 26240 - ROW, ROW)
        zeros = view(region, 26240, DIM)
        g_flat = g_sb[:, :, :, :, :].rearrange("p a b c d -> p (a b c d)")
        v_flat = v_sb[:, :, :, :].rearrange("p a b c -> p (a b c)")
        XS = 3
        xe = [view(g_flat, s * GRP * ROW, GRP, ROW) for s in range(XS)]
        xt = [view(v_flat, s * 512, 2, CH, CAP) for s in range(2)]
        sg = [view(v_flat, 1024 + s * 256, 2, FF) for s in range(2)]
        hw = [view(v_flat, 1536 + s * 256, 2, FF) for s in range(2)]
        ht = [view(v_flat, 2048 + s * 256, 2, CAP) for s in range(2)]
        YS = 4
        ysb = [view(v_flat, 2560 + s * 512, 2, DIM) for s in range(YS)]
        sg_sh = view(v_flat, 4608, 512)
        SLOT = GRP * ROW
        acc = [view(g_flat, 2 * SLOT, TILES, DIM), view(g_flat, SLOT, TILES, DIM), view(g_flat, 0, TILES, DIM),
               view(v_flat, 5120, TILES, DIM)]

        at = [0]

        def take(*dims):
            n = 1
            for d in dims:
                n *= d
            v = view(small, at[0], *dims)
            at[0] += n
            return v
        rmax, rsum = take(2, HEADS), take(2, HEADS)
        stats, mv = take(TILES, 6), take(TILES, 2)
        veps, lnv, rs0, rs1, rstd = take(TILES), take(TILES), take(TILES), take(TILES), take(TILES)
        ebias = take(EXP)
        el, sc = take(EXP), take(EXP)
        s0 = take(EXP + 1)
        pair = take(GRP, EPG * (EPG - 1) // 2)
        gsum = take(2 * GRP)
        top4 = take(2 * 8)
        msk = take(EXP)
        rep = take(EXP + 1)
        top8, key8 = take(8), take(TOPK)
        wsum = take(TILES)
        mark_sb = take(1)
        key, keys = take(EXP), take(EXP)
        shw = view(region, 25536, 2 * CH, FF)
        shd = view(region, 24064, DIM)
        rw = view(region, 25216, CH, EXP)
        pick16 = region[:, 24320:24576].bitcast(f16).rearrange("p (t e) -> p t e", e=EXP)
        assert at[0] <= 2048
        rows8 = sb("rows8", [P, TILES * TOPK], u32)
        ident = const[:, C_IDENT:C_IDENT + P]

        bank = [ctx.enter_context(nc.psum_tensor(f"bank{i}", [P, 512], f32)) for i in range(8)]

        names = ("ld_const ld_x ld_ctx ld_wqr0 ld_wqr1 ld_wkr ld_wkcq0 ld_wkcq1 ld_wq0 ld_wq1 ld_wkv ld_wo ld_router ld_sh ld_empty "
                 "wkr_zero near_spread filled zeroed ctx_roped bd_zero zero_ok prep_mm prep_act prep_dve stats1 rstd1 hn1 "
                 "scores nmax expd probs pt pt_sb attn x_ok stats2 rstd2 hn2 "
                 "hn2T hn2T_sb logits elog pick slot_read rows weights spread "
                 "sh_gu sh_act sh_h sh_dn sh_added "
                 "tx xt_ok gu silu h th ht_ok dn y_ok "
                 "added outd d_chain a_chain").split()
        S = {n: sem(n) for n in names}
        s_w = [sem(f"ld_expert{s}") for s in range(WSLOTS)]
        s_xe = [[sem(f"ld_rows{s}_{pr}") for pr in range(4)] for s in range(XS)]
        s_sum = [sem(f"summed{s}") for s in range(NSUM)]
        s_acc = [[sem(f"ld_sums{s}_{q}") for q in range(OUTS)] for s in range(NSUM)]

        def sums_after(m, s):
            return 16 * TABLE[:max(m, 0)].count(s)

        block = ctx.enter_context(nc.Block())

        TPV = 2 * PAIRS
        items = ([("A", n) for n in range(2)] + [("K", 0)] + [("E", n) for n in range(2)]
                 + [("C", n) for n in range(4)] + [("G", n) for n in range(12)]
                 + [("H", n) for n in range(4)] + [("G", n) for n in range(12, 16)]
                 + [("F", n) for n in range(4)] + [("V", n) for n in range(TPV)])
        NI = len(items)
        NV = NI - 4 - TPV
        bank_of = [n % 8 if n < NV else 4 + (n - NV) % 4 for n in range(NI)]
        by_act = [n < 13 or n % 2 == 0 for n, it in enumerate(items[:NV])]
        by_act += [j % 3 == 0 for j in range(4 + TPV)]

        def out_by(n):
            a = sum(by_act[:n + 1])
            return a, n + 1 - a

        def move_out(eng, kind, j, n, copy, done):
            b = bank[bank_of[n]]
            if kind == "K":
                eng.wait_ge(S["bd_zero"], 1)
                src = b[:, 0:256].rearrange("p (b k) -> p b k", b=BATCH)
                copy(bd[0:DC, :, 0, :], src[0:DC])
                copy(bd[DC:P, :, 1, :], src[DC:P]).then_inc(done, 1)
            if kind == "A":
                copy(a_sb[:, 4 * j:4 * j + 4, :], b[:, :].rearrange("p (a k) -> p a k", a=4)).then_inc(done, 1)
            if kind == "E":
                copy(e_sb[:, 8 * j:8 * j + 8, :], b[:, :].rearrange("p (h d) -> p h d", d=DC)).then_inc(done, 1)
            if kind == "C":
                copy(c_sb[:, 2 * j:2 * j + 2, :], b[:, :].rearrange("p (a m) -> p a m", a=2)).then_inc(done, 1)
            if kind == "F":
                copy(f_sb[:, 2 * j:2 * j + 2, :], b[:, :].rearrange("p (a m) -> p a m", a=2)).then_inc(done, 1)
            if kind == "H":
                copy(hnT[:, :, 2 * j * P:(2 * j + 2) * P],
                     b[:, :].rearrange("p (c m) -> p c m", c=CH)).then_inc(done, 1)
            if kind == "G":
                copy(g_sb[:, j % 2, :, j // 2, :], b[:, :].rearrange("p (b k) -> p b k", b=BATCH)).then_inc(done, 1)
            if kind == "V":
                copy(v_sb[:, 2 * (j % 2):2 * (j % 2) + 2, j // 2, :],
                     b[:, :].rearrange("p (b m) -> p b m", b=2)).then_inc(done, 1)

        @block.sync
        def _(sp):
            for j in range(2):
                hs = slice(8 * j, 8 * j + 8)
                sp.dma_start(wqr[0:QP, hs, :, :], a["wqr"][:, hs, :, :]).then_inc(S[f"ld_wqr{j}"], 16)
                sp.dma_start(wkcq[0:QP, hs, :, :], a["wkcq"][:, hs, :, :]).then_inc(S[f"ld_wkcq{j}"], 16)
                if j == 0:
                    sp.dma_start(ctx_sb[:, :, :], a["ctx"]).then_inc(S["ld_ctx"], 16)
                    sp.dma_start(const[:, :], a["const"]).then_inc(S["ld_const"], 16)
            sp.wait_ge(S["wkr_zero"], 1)
            for h2 in range(2):
                hs = slice(h2 * RK, (h2 + 1) * RK)
                sp.dma_start(wkr[hs, :, h2, :], a["wkr"][hs]).then_inc(S["ld_wkr"], 16)
            for j in range(2):
                hs = slice(8 * j, 8 * j + 8)
                sp.dma_start(wq[:, hs, :], a["wq"][:, hs, :]).then_inc(S[f"ld_wq{j}"], 16)
            sp.dma_start(x[:, :, :], a["x"].rearrange("(t p) m -> p t m", p=P)).then_inc(S["ld_x"], 16)
            sp.dma_start(wkv[:, :, :], a["wkv"]).then_inc(S["ld_wkv"], 16)
            sp.dma_start(wo[:, :, :], a["wo"]).then_inc(S["ld_wo"], 16)
            sp.dma_start(rw[:, :, :], a["rw"]).then_inc(S["ld_router"], 16)
            sp.dma_start(ebias, a["ebias"]).then_inc(S["ld_router"], 16)
            sp.dma_start(shw[:, :, :], a["shw"]).then_inc(S["ld_sh"], 16)
            sp.dma_start(empty, a["empty"]).then_inc(S["ld_empty"], 16)
            sp.wait_ge(S["ld_empty"], 16)
            for i in range(EPG):
                sp.dma_start(xe_table[i * GRP * CAP:(i + 1) * GRP * CAP, :].rearrange("(s g) m -> s g m", g=GRP),
                             empty.unsqueeze(1).to_broadcast([P, GRP, ROW])).then_inc(S["filled"], 16)
            sp.wait_ge(S["zero_ok"], 1)
            for s in range(NSUM):
                sp.dma_start(sums[s].rearrange("(t p) m -> p t m", p=P),
                             zeros.unsqueeze(1).to_broadcast([P, TILES + 1, DIM])).then_inc(S["zeroed"], 16)

            def load_weights(n):
                i, pr = n // 4, n % 4
                s, gs = i % WSLOTS, slice(2 * pr, 2 * pr + 2)
                sp.dma_start(wgu_sb[s][:, gs], a["wgu"][i, :, gs]).then_inc(s_w[s], 16)
                sp.dma_start(wdn_sb[s][0:FF, gs], a["wdn"][i, :, gs]).then_inc(s_w[s], 16)

            def load_rows(n):
                i, pr = n // 4, n % 4
                gs = slice(2 * pr, 2 * pr + 2)
                src = xe_table[i * GRP * CAP:(i + 1) * GRP * CAP, :].rearrange("(s g) m -> s g m", g=GRP)
                sp.dma_start(xe[i % XS][:, gs, :], src[:, gs, :]).then_inc(s_xe[i % XS][pr], 16)

            sp.wait_ge(S["prep_mm"], NI)
            sp.dma_start(shd[0:FF, :], a["shd"]).then_inc(S["ld_sh"], 16)
            for n in range(3 * 4):
                load_weights(n)
            sp.wait_ge(S["attn"], TILES)
            for n in range(3 * 4, 4 * 4):
                load_weights(n)
            sp.wait_ge(S["spread"], 16 * TILES * TOPK)
            for n in range(4 * XS):
                load_rows(n)
            LAG = 3
            for n in range(EXP // 2):
                if n + 4 * WSLOTS < EXP // 2:
                    sp.wait_ge(S["dn"], n + 1)
                    load_weights(n + 4 * WSLOTS)
                m = n - LAG
                if m >= 0 and m + 4 * XS < EXP // 2:
                    for s in range(NSUM):
                        sp.wait_ge(s_sum[s], sums_after(2 * m + 2, s))
                    load_rows(m + 4 * XS)
            for s in CLOSING:
                if s != CLOSING[0]:
                    for r in range(NSUM):
                        sp.wait_ge(s_sum[r], sums_after(EXP - EPG, r))
                sp.wait_ge(s_sum[s], sums_after(EXP, s))
                for q in range(OUTS):
                    ts = slice(q * TILES // OUTS, (q + 1) * TILES // OUTS)
                    sp.dma_start(acc[s][:, ts, :],
                                 sums[s][0:TOK, :].rearrange("(t p) m -> p t m", p=P)[:, ts, :]).then_inc(s_acc[s][q], 16)
            for q in range(OUTS):
                ts = slice(q * TILES // OUTS, (q + 1) * TILES // OUTS)
                sp.wait_ge(S["added"], (NSUM - 1) * OUTS + q + 1)
                sp.dma_start(out.rearrange("(t p) m -> p t m", p=P)[:, ts, :], x[:, ts, :]).then_inc(S["outd"], 16)
            sp.wait_ge(S["outd"], 16 * OUTS)

        @block.tensor
        def _(pe):
            mm, tr = nc.tensor.matmul, nc.tensor.transpose

            def settle(n):
                act, dve = out_by(n)
                pe.wait_ge(S["prep_act"], act)
                if dve:
                    pe.wait_ge(S["prep_dve"], dve)
            def scores(t):
                if t >= 2:
                    pe.wait_ge(S["expd"], t - 1)
                for half in range(2):
                    if t == 0:
                        settle(NV - 5 if half == 0 else NV - 1)
                    for c in range(CH):
                        last = mm(bank[2 * (t % 2) + half][:, :], hnT[:, c, t * P:(t + 1) * P],
                                  g_sb[:, c, t // TPB, 4 * half:4 * half + 4, :].rearrange("p a b -> p (a b)"),
                                  start=(c == 0), stop=(c == CH - 1))
                last.then_inc(S["scores"], 1)

            def warm(count):
                for w in range(count):
                    mm(bank[0][:, :], bd[:, 0].rearrange("p h k -> p (h k)"),
                       bd[:, :, :, :].rearrange("p b h k -> p (b h k)"), start=True, stop=True)

            pe.wait_ge(S["bd_zero"], 1)
            warm(3)
            seen = set()
            for n, (kind, j) in enumerate(items):
                b = bank[bank_of[n]]
                if n == NV:
                    scores(0)
                if n == NV + 8:
                    scores(1)
                if n >= 8:
                    settle(n - 8 if n < NV else max(n - 4, NV - 1))
                first = kind not in seen
                seen.add(kind)
                if kind == "K":
                    pe.wait_ge(S["ctx_roped"], 1)
                    pe.wait_ge(S["ld_const"], 16)
                    for c in range(2):
                        last = tr(b[:, c * P:(c + 1) * P], kvr[:, c, :], ident)
                if kind == "A":
                    pe.wait_ge(S[f"ld_wqr{j}"], 16)
                    pe.wait_ge(S[f"ld_wkcq{j}"], 16)
                    for q in range(4):
                        for c in range(QC):
                            for h2 in range(2):
                                h = 8 * j + 2 * q + h2
                                last = mm(b[h2 * RK:(h2 + 1) * RK, q * HK:(q + 1) * HK], wqr[0:QP, h, c, :],
                                          wkcq[0:QP, h, c, :], start=(c == 0), stop=(c == QC - 1))
                if kind == "E":
                    if first:
                        pe.wait_ge(S["ld_wkr"], 32)
                    settle(items.index(("A", j)))
                    for q in range(4):
                        p = 4 * j + q
                        last = mm(b[:, q * P:(q + 1) * P], a_sb[:, p, :], wkr[:, p, :, :].rearrange("p a d -> p (a d)"),
                                  start=True, stop=True)
                if kind == "C":
                    settle(items.index(("E", j // 2)))
                    pe.wait_ge(S[f"ld_wq{j // 2}"], 16)
                    for q in range(2):
                        for h2 in range(2):
                            h = 4 * j + 2 * q + h2
                            last = mm(b[h2 * DC:(h2 + 1) * DC, q * DIM:(q + 1) * DIM], e_sb[:, h, :], wq[:, h, :],
                                      start=True, stop=True)
                if kind == "F":
                    if first:
                        pe.wait_ge(S["ld_wkv"], 16)
                        pe.wait_ge(S["ld_wo"], 16)
                    for q in range(2):
                        for h2 in range(2):
                            h = 4 * j + 2 * q + h2
                            last = mm(b[h2 * DC:(h2 + 1) * DC, q * DIM:(q + 1) * DIM], wkv[:, h, :], wo[:, h, :],
                                      start=True, stop=True)
                if kind == "H":
                    pe.wait_ge(S["hn1"], 2 * j + 2)
                    for q in range(2):
                        for c in range(CH):
                            o = (c * 2 + q) * P
                            last = tr(b[:, o:o + P], hn[:, 2 * j + q, c * P:(c + 1) * P], ident)
                if kind == "G":
                    p, c = j // 2, j % 2
                    settle(items.index(("C", p // 2)))
                    last = mm(b[:, :], c_sb[:, p, c * P:(c + 1) * P],
                              bd[:, :, :, :].rearrange("p b h k -> p (b h k)"), start=True, stop=True)
                if kind == "V":
                    p, bp = j // 2, j % 2
                    for q in range(2):
                        last = mm(b[:, q * DIM:(q + 1) * DIM],
                                  bd[:, 2 * bp + q, :, :].rearrange("p h k -> p (h k)"),
                                  f_sb[:, p, :], start=True, stop=True)
                last.then_inc(S["prep_mm"], 1)

            def turn_probs(t):
                pe.wait_ge(S["probs"], t + 1)
                if t:
                    pe.wait_ge(S["pt_sb"], 2 * t)
                for half in range(2):
                    if t == 0:
                        settle(NI - 4 + half)
                    for q in range(4):
                        p = 4 * half + q
                        last = tr(bank[4 + half][:, q * P:(q + 1) * P], p_sb[:, t % 2, p * P:(p + 1) * P], ident)
                    last.then_inc(S["pt"], 1)

            def attend(t, half):
                if half == 0 and t:
                    pe.wait_ge(S["x_ok"], t)
                if half == 0 and t >= 3:
                    pe.wait_ge(S["slot_read"], t - 2)
                if t == 0:
                    settle(NI - 1)
                pe.wait_ge(S["pt_sb"], 2 * t + 1 + half)
                for p in range(4 * half, 4 * half + 4):
                    last = mm(bank[6][:, 0:DIM], pt_sb[:, t % 2, p, :], v_sb[:, t // TPB, p, :],
                              start=(p == 0), stop=(p == PAIRS - 1))
                return last

            turned, routed = [0], [0]

            def bank7_read():
                if turned[0]:
                    pe.wait_ge(S["hn2T_sb"], turned[0])
                if routed[0]:
                    pe.wait_ge(S["elog"], routed[0])

            def turn_hn2(t):
                pe.wait_ge(S["hn2"], t + 1)
                bank7_read()
                for c in range(CH):
                    last = tr(bank[7][:, c * P:(c + 1) * P], hn[:, t, c * P:(c + 1) * P], ident)
                last.then_inc(S["hn2T"], 1)
                turned[0] = t + 1

            def route_logits(t):
                bank7_read()
                if t == 0:
                    pe.wait_ge(S["ld_router"], 32)
                for c in range(CH):
                    last = mm(bank[7][:, 256:256 + EXP], hnT[:, c, t * P:(t + 1) * P], rw[:, c, :],
                              start=(c == 0), stop=(c == CH - 1))
                last.then_inc(S["logits"], 1)
                routed[0] = t + 1

            def slot_numbers(t):
                pe.wait_ge(S["pick"], t + 1)
                if t >= TILES - 2:
                    pe.wait_ge(S["slot_read"], t)
                    pe.wait_ge(S["x_ok"], TILES)
                o = bank[6][:, 256:256 + EXP]
                last = mm(o, near16[:, :], pick16[:, t, :], start=True, stop=(t == 0))
                for q in range(t):
                    last = mm(o, ones16[:, :], pick16[:, q, :], start=False, stop=(q == t - 1))
                return last

            def shared_gate_up(half):
                if half == 0:
                    pe.wait_ge(S["ld_sh"], 32)
                    pe.wait_ge(S["expd"], TILES)
                pe.wait_ge(S["hn2T_sb"], 4 * half + 4)
                for gu in range(2):
                    for c in range(CH):
                        last = mm(bank[2 * half + gu][0:FF, :], shw[:, gu * CH + c, :],
                                  hnT[:, c, half * 512:(half + 1) * 512], start=(c == 0), stop=(c == CH - 1))
                last.then_inc(S["sh_gu"], 1)

            for t in range(TILES + 2):
                if t < TILES:
                    turn_probs(t)
                if t + 2 < TILES:
                    scores(t + 2)
                if t < TILES:
                    last = attend(t, 0)
                if t >= TILES:
                    shared_gate_up(t - TILES)
                if 1 <= t <= TILES:
                    turn_hn2(t - 1)
                if t < TILES:
                    last = attend(t, 1)
                if t == TILES:
                    route_logits(t - 1)
                if t >= 2:
                    last = slot_numbers(t - 2)
                last.then_inc(S["attn"], 1)
                if 1 <= t < TILES:
                    route_logits(t - 1)
            for t in range(TILES):
                if t % 4 == 0:
                    pe.wait_ge(S["sh_h"], t // 4 + 1)
                if t == 0:
                    pe.wait_ge(S["pt_sb"], 2 * TILES)
                b = bank[(4, 5, 2, 3)[t // 2]]
                last = mm(b[:, (t % 2) * DIM:(t % 2 + 1) * DIM], h_sh[0:FF, t * P:(t + 1) * P], shd[0:FF, :],
                          start=True, stop=True)
                if t % 2:
                    last.then_inc(S["sh_dn"], 1)

            def turn_rows(n):
                i, pr = n // 4, n % 4
                pe.wait_ge(s_xe[i % XS][pr], 16 * (i // XS + 1))
                if n >= 2:
                    pe.wait_ge(S["xt_ok"], n - 1)
                for q in range(2):
                    for c in range(CH):
                        last = tr(bank[n % 2][:, (q * CH + c) * P:(q * CH + c + 1) * P],
                                  xe[i % XS][:, 2 * pr + q, c * P:(c + 1) * P], ident)
                last.then_inc(S["tx"], 1)

            def gate_up(n):
                i, pr = n // 4, n % 4
                if pr == 0:
                    pe.wait_ge(s_w[i % WSLOTS], 16 * EPG * (i // WSLOTS + 1))
                pe.wait_ge(S["xt_ok"], n + 1)
                if n >= 2:
                    pe.wait_ge(S["h"], n - 1)
                for q in range(2):
                    for c in range(CH):
                        last = mm(bank[2 + n % 2][:, q * 2 * FF:(q + 1) * 2 * FF], xt[n % 2][:, q, c, :],
                                  wgu_sb[i % WSLOTS][:, 2 * pr + q, c, :], start=(c == 0), stop=(c == CH - 1))
                last.then_inc(S["gu"], 1)

            def turn_hidden(n):
                pe.wait_ge(S["h"], n + 1)
                if n >= 2:
                    pe.wait_ge(S["ht_ok"], n - 1)
                for q in range(2):
                    last = tr(bank[4 + n % 2][0:FF, q * CAP:(q + 1) * CAP], hw[n % 2][:, q, :], ident)
                last.then_inc(S["th"], 1)

            def down(n):
                i, pr = n // 4, n % 4
                pe.wait_ge(S["ht_ok"], n + 1)
                if n >= 2:
                    pe.wait_ge(S["y_ok"], n - 1)
                for q in range(2):
                    last = mm(bank[6 + n % 2][:, q * DIM:(q + 1) * DIM], ht[n % 2][0:FF, q, :],
                              wdn_sb[i % WSLOTS][0:FF, 2 * pr + q, :], start=True, stop=True)
                last.then_inc(S["dn"], 1)

            pe.wait_ge(S["sh_added"], TILES // 2)
            pe.wait_ge(S["slot_read"], TILES)
            pe.wait_ge(S["near_spread"], 1)
            warm(7)
            NP = EXP // 2
            for n in range(NP + 3):
                if n < NP:
                    turn_rows(n)
                if 2 <= n < NP + 2:
                    turn_hidden(n - 2)
                if 1 <= n < NP + 1:
                    gate_up(n - 1)
                if n >= 3:
                    down(n - 3)

        @block.scalar
        def _(act):
            A = nc.scalar.activation
            nc.scalar.preload_act_table_set("natural_log_exp_and_others")

            def copy_out(o, i):
                return A(o, i, ACT.Copy)

            def rsqrt_seed(ts, ready, n, done):
                act.wait_ge(ready, n)
                A(lnv[:, ts], veps[:, ts], ACT.Ln, scale=-2.0).then_inc(S["a_chain"], 1)
                act.wait_ge(S["a_chain"], n)
                A(rs0[:, ts], lnv[:, ts], ACT.Exp, scale=-0.5).then_inc(done, 1)

            def exp_scores(t, h0=0, h1=HEADS):
                if h0 == 0:
                    act.wait_ge(S["nmax"], t + 1)
                    if t >= 2:
                        act.wait_ge(S["pt"], 2 * (t - 1))
                for h in range(h0, h1):
                    last = A(p_sb[:, t % 2, h * KEYS:(h + 1) * KEYS],
                             bank[2 * (t % 2) + h // 8][:, h % 8 * KEYS:(h % 8 + 1) * KEYS], ACT.Exp,
                             bias=rmax[:, t % 2, h:h + 1], accum_out=rsum[:, t % 2, h:h + 1])
                if h1 == HEADS:
                    last.then_inc(S["expd"], 1)

            for n, (kind, j) in enumerate(items):
                if n == 11:
                    rsqrt_seed(slice(0, TILES), S["stats1"], 1, S["rstd1"])
                if by_act[n]:
                    act.wait_ge(S["prep_mm"], n + 1)
                    move_out(act, kind, j, n, copy_out, S["prep_act"])
                if n >= NV and by_act[n]:
                    q = (n - NV) // 3
                    if q < 6:
                        exp_scores(q // 4, 4 * (q % 4), 4 * (q % 4) + 4)
            exp_scores(1, 8)

            for t in range(TILES + 1):
                if t < TILES:
                    for half in range(2):
                        act.wait_ge(S["pt"], 2 * t + half + 1)
                        if t >= 2:
                            act.wait_ge(S["attn"], t - 1)
                        A(pt_sb[:, t % 2, 4 * half:4 * half + 4, :],
                          bank[4 + half][:, :].rearrange("p (a b) -> p a b", b=P), ACT.Copy).then_inc(S["pt_sb"], 1)
                if t >= 1:
                    act.wait_ge(S["stats2"], t)
                    A(lnv[:, t - 1:t], veps[:, t - 1:t], ACT.Ln, scale=-2.0).then_inc(S["a_chain"], 1)
                    act.wait_ge(S["a_chain"], t + 1)
                    A(rs0[:, t - 1:t], lnv[:, t - 1:t], ACT.Exp, scale=-0.5).then_inc(S["rstd2"], 1)
                if t >= 1:
                    act.wait_ge(S["hn2T"], t)
                    act.wait_ge(S["scores"], t)
                    A(hnT[:, :, (t - 1) * P:t * P], bank[7][:, 0:DIM].rearrange("p (c q) -> p c q", c=CH),
                      ACT.Copy).then_inc(S["hn2T_sb"], 1)
                if t + 2 < TILES:
                    exp_scores(t + 2, 0, 8)
                if t >= 1:
                    act.wait_ge(S["logits"], t)
                    if t >= 2:
                        act.wait_ge(S["pick"], t - 1)
                    A(el, bank[7][:, 256:256 + EXP], ACT.Exp, scale=-1.0).then_inc(S["elog"], 1)
                if t + 2 < TILES:
                    exp_scores(t + 2, 8, 16)
            for half in range(2):
                act.wait_ge(S["sh_gu"], half + 1)
                if half:
                    act.wait_ge(S["sh_h"], half)
                A(sg_sh[0:FF, :], bank[2 * half][0:FF, :], ACT.Silu).then_inc(S["sh_act"], 1)

            def rows_out(n):
                act.wait_ge(S["tx"], n + 1)
                if n >= 2:
                    act.wait_ge(S["gu"], n - 1)
                A(xt[n % 2], bank[n % 2][:, :].rearrange("p (q c s) -> p q c s", q=2, c=CH),
                  ACT.Copy).then_inc(S["xt_ok"], 1)

            def hidden_out(n):
                act.wait_ge(S["th"], n + 1)
                if n >= 2:
                    act.wait_ge(S["dn"], n - 1)
                A(ht[n % 2][0:FF], bank[4 + n % 2][0:FF, 0:2 * CAP].rearrange("p (q s) -> p q s", q=2),
                  ACT.Copy).then_inc(S["ht_ok"], 1)

            def silu(n):
                act.wait_ge(S["gu"], n + 1)
                if n >= 2:
                    act.wait_ge(S["h"], n - 1)
                A(sg[n % 2], bank[2 + n % 2][:, 0:4 * FF].rearrange("p (q u f) -> p q u f", q=2, u=2)[:, :, 0, :],
                  ACT.Silu).then_inc(S["silu"], 1)
            NP = EXP // 2
            for n in range(NP + 2):
                if n < NP:
                    rows_out(n)
                if n >= 2:
                    hidden_out(n - 2)
                if 1 <= n < NP + 1:
                    silu(n - 1)

        @block.vector
        def _(dve):
            V = nc.vector
            n_chain = [0]

            def then(ins):
                n_chain[0] += 1
                ins.then_inc(S["d_chain"], 1)
                dve.wait_ge(S["d_chain"], n_chain[0])

            def mark(ins):
                n_chain[0] += 1
                ins.then_inc(S["d_chain"], 1)
                return n_chain[0]

            def after(value):
                dve.wait_ge(S["d_chain"], value)

            V.memset(bd[:, :, :, :], 0.0).then_inc(S["bd_zero"], 1)
            V.memset(wkr, 0.0).then_inc(S["wkr_zero"], 1)
            V.memset(zeros, 0.0).then_inc(S["zero_ok"], 1)
            V.memset(ones16[:, :], 1.0)
            V.memset(hn[:, :, C_NUM:ROW], 0.0)
            V.memset(top4, BIG)
            V.memset(s0[:, EXP:EXP + 1], 1e-20)
            V.memset(rep[:, EXP:EXP + 1], -BIG)
            then(V.memset(gsum, BIG))
            dve.wait_ge(S["ld_ctx"], 16)
            dve.wait_ge(S["ld_const"], 16)
            V.tensor_copy(near16[:, :], const[:, C_TRI:C_TRI + P])
            V.tensor_copy(hn[:, :, C_NUM].bitcast(u32), const[:, C_TOK:C_TOK + TILES])
            cosv, sinv = const[:, C_COS:C_COS + DC], const[:, C_SIN:C_SIN + DC]
            hd = DC // 2
            for c in range(2):
                V.tensor_tensor(kvt[:, c, 0:hd], ctx_sb[:, c, hd:DC], sinv[:, 0:hd], ALU.mult)
                V.tensor_tensor(kvt[:, c, hd:DC], ctx_sb[:, c, 0:hd], sinv[:, hd:DC], ALU.mult)
                then(V.tensor_tensor(kvr[:, c, 0:DC], ctx_sb[:, c, :], cosv, ALU.mult))
                then(V.tensor_tensor(kvr[:, c, 0:DC], kvr[:, c, 0:DC], kvt[:, c, :], ALU.add))
                last = V.tensor_copy(kvr[:, c, DC:2 * DC], kvr[:, c, 0:DC])
            last.then_inc(S["ctx_roped"], 1)

            def ln_stats(t):
                then(V.bn_stats(stats[:, t, :], x[:, t, :]))
                return V.bn_aggr(mv[:, t, :], stats[:, t, :])

            def refine(ts):
                then(V.tensor_tensor(rs1[:, ts], rs0[:, ts], veps[:, ts], ALU.mult))
                then(V.tensor_tensor(rs1[:, ts], rs1[:, ts], rs0[:, ts], ALU.mult))
                then(V.scalar_tensor_tensor(rstd[:, ts], rs1[:, ts], 1.5, rs0[:, ts], ALU.add, ALU.mult))

            dve.wait_ge(S["ld_x"], 16)
            for t in range(TILES):
                last = ln_stats(t)
            then(last)
            V.tensor_scalar(veps, mv[:, :, 1], EPS, -0.5, ALU.add, ALU.mult).then_inc(S["stats1"], 1)
            dve.wait_ge(S["rstd1"], 1)
            refine(slice(0, TILES))
            for t in range(TILES):
                V.tensor_scalar(hn[:, t, 0:DIM], x[:, t, :], mv[:, t, 0:1], rstd[:, t:t + 1],
                                ALU.subtract, ALU.mult).then_inc(S["hn1"], 1)

            def softmax_max(t, half):
                if half == 0:
                    dve.wait_ge(S["scores"], t + 1)
                    if t >= 2:
                        dve.wait_ge(S["expd"], t - 1)
                last = V.tensor_reduce(rmax[:, t % 2, 8 * half:8 * half + 8],
                                       bank[2 * (t % 2) + half][:, :].rearrange("p (h k) -> p h k", h=8),
                                       AX.X, ALU.max, negate=True)
                if half == 1:
                    last.then_inc(S["nmax"], 1)

            heads = p_sb.rearrange("p b (h k) -> p b h k", h=HEADS)
            for n, (kind, j) in enumerate(items):
                if not by_act[n]:
                    dve.wait_ge(S["prep_mm"], n + 1)
                    move_out(dve, kind, j, n, V.tensor_copy, S["prep_dve"])
                if n == NV:
                    softmax_max(0, 0)
                    softmax_max(0, 1)
                if n == NV + 13:
                    dve.wait_ge(S["expd"], 1)
                    then(V.reciprocal(rsum[:, 0, :], rsum[:, 0, :]))
                    V.tensor_tensor(heads[:, 0], heads[:, 0],
                                    rsum[:, 0, :].unsqueeze(2).to_broadcast([P, HEADS, KEYS]),
                                    ALU.mult).then_inc(S["probs"], 1)
                if n == NV + 8:
                    softmax_max(1, 0)
                    softmax_max(1, 1)

            for t in range(TILES + 3):
                at1 = t - 1 if 1 <= t <= TILES else None
                pk = t - 2 if 2 <= t < TILES + 2 else None
                pl = t - 3 if t >= 3 else None
                nm = t + 1 if t + 1 < TILES else None
                mx = t + 2 if t + 2 < TILES else None
                if t:
                    dve.wait_ge(S["attn"], t)
                if pl is not None:
                    num = bank[6][:, 256:256 + EXP]
                    q = mark(V.scalar_tensor_tensor(key, num, -float(GRP), const[:, C_KEY:C_KEY + EXP],
                                                    ALU.mult, ALU.add))
                if at1 is not None:
                    V.tensor_tensor(x[:, at1, :], x[:, at1, :], bank[6][:, 0:DIM], ALU.add).then_inc(S["x_ok"], 1)
                if pl is not None:
                    after(q)
                    V.scalar_tensor_tensor(keys, num, FAR, key, ALU.is_lt, ALU.mult).then_inc(S["slot_read"], 1)
                if at1 is not None:
                    dve.wait_ge(S["x_ok"], at1 + 1)
                    a1 = mark(V.bn_stats(stats[:, at1, :], x[:, at1, :]))
                if pl is not None:
                    dve.wait_ge(S["slot_read"], pl + 1)
                    q = mark(V.max(key8, keys))
                if at1 is not None:
                    after(a1)
                    a1 = mark(V.bn_aggr(mv[:, at1, :], stats[:, at1, :]))
                if pl is not None:
                    after(q)
                    V.tensor_scalar(rows8[:, pl * TOPK:(pl + 1) * TOPK], key8, -1.0, NOROW, ALU.mult, ALU.add
                                    ).then_inc(S["rows"], 1)
                if at1 is not None:
                    after(a1)
                    V.tensor_scalar(veps[:, at1:at1 + 1], mv[:, at1, 1:2], EPS, -0.5, ALU.add, ALU.mult
                                    ).then_inc(S["stats2"], 1)
                if pk is not None:
                    dve.wait_ge(S["elog"], pk + 1)
                    p = mark(V.tensor_scalar_add(s0[:, 0:EXP], el, 1.0))
                if pk is not None:
                    after(p)
                    p = mark(V.reciprocal(s0[:, 0:EXP], s0[:, 0:EXP]))
                if pk is not None:
                    after(p)
                    p = mark(V.tensor_tensor(sc, s0[:, 0:EXP], ebias, ALU.add))
                if pk is not None:
                    after(p)
                    g = sc.rearrange("p (g e) -> p g e", g=GRP)
                    o = 0
                    for d in range(1, EPG):
                        last = V.tensor_tensor(pair[:, :, o:o + EPG - d], g[:, :, 0:EPG - d], g[:, :, d:EPG], ALU.add)
                        o += EPG - d
                    p = mark(last)
                if nm is not None:
                    dve.wait_ge(S["expd"], nm + 1)
                    n = mark(V.reciprocal(rsum[:, nm % 2, :], rsum[:, nm % 2, :]))
                if pk is not None:
                    after(p)
                    p = mark(V.tensor_reduce(gsum[:, 0:GRP], pair, AX.X, ALU.max))
                if nm is not None:
                    after(n)
                    V.tensor_tensor(heads[:, nm % 2], heads[:, nm % 2],
                                    rsum[:, nm % 2, :].unsqueeze(2).to_broadcast([P, HEADS, KEYS]),
                                    ALU.mult).then_inc(S["probs"], 1)
                if at1 is not None:
                    dve.wait_ge(S["rstd2"], at1 + 1)
                    ts = slice(at1, at1 + 1)
                    a1 = mark(V.scalar_tensor_tensor(rs1[:, ts], rs0[:, ts], veps[:, ts], rs0[:, ts],
                                                     ALU.mult, ALU.mult))
                if pk is not None:
                    after(p)
                    p = mark(V.max(top4[:, 0:8], gsum[:, 0:GRP]))
                if at1 is not None:
                    after(a1)
                    a1 = mark(V.scalar_tensor_tensor(rstd[:, ts], rs1[:, ts], 1.5, rs0[:, ts], ALU.add, ALU.mult))
                if pk is not None:
                    after(p)
                    p = mark(V.match_replace(rep[:, 0:2 * GRP], top4.rearrange("p (a b) -> p a b", b=8)[:, :, 0:TOPG],
                                             gsum, -BIG))
                if at1 is not None:
                    after(a1)
                    V.tensor_scalar(hn[:, at1, 0:DIM], x[:, at1, :], mv[:, at1, 0:1], rstd[:, at1:at1 + 1],
                                    ALU.subtract, ALU.mult).then_inc(S["hn2"], 1)
                if pk is not None:
                    after(p)
                    p = mark(V.scalar_tensor_tensor(msk.rearrange("p (g e) -> p g e", g=GRP),
                                                    rep[:, 0:GRP].unsqueeze(2).to_broadcast([P, GRP, EPG]), -BIG, g,
                                                    ALU.is_equal, ALU.mult))
                if mx is not None:
                    softmax_max(mx, 0)
                if pk is not None:
                    after(p)
                    p = mark(V.max(top8, msk))
                if mx is not None:
                    softmax_max(mx, 1)
                if pk is not None:
                    after(p)
                    p = mark(V.match_replace(rep[:, 0:EXP], top8, msk, -BIG))
                if pk is not None:
                    after(p)
                    V.tensor_single_scalar(pick16[:, pk, :], rep[:, 0:EXP], -BIG, ALU.is_equal).then_inc(S["pick"], 1)
                    then(V.scalar_tensor_tensor(s0, rep, -BIG, s0, ALU.is_equal, ALU.mult,
                                                accum_out=wsum[:, pk:pk + 1]))
                    then(V.reciprocal(wsum[:, pk:pk + 1], wsum[:, pk:pk + 1]))
                    V.tensor_scalar(hn[:, pk, DIM:DIM + EXP], s0[:, 0:EXP], wsum[:, pk:pk + 1], SCALE,
                                    ALU.mult, ALU.mult).then_inc(S["weights"], 1)

            for half in range(2):
                dve.wait_ge(S["sh_act"], half + 1)
                V.tensor_tensor(h_sh[0:FF, half * 512:(half + 1) * 512], sg_sh[0:FF, :], bank[2 * half + 1][0:FF, :],
                                ALU.mult).then_inc(S["sh_h"], 1)
            for j in range(TILES // 2):
                dve.wait_ge(S["sh_dn"], j + 1)
                b = bank[(4, 5, 2, 3)[j]]
                V.tensor_tensor(x[:, 2 * j:2 * j + 2, :], x[:, 2 * j:2 * j + 2, :],
                                b[:, :].rearrange("p (t m) -> p t m", t=2), ALU.add).then_inc(S["sh_added"], 1)

            def hidden(n):
                i, pr = n // 4, n % 4
                dve.wait_ge(S["silu"], n + 1)
                if n >= 2:
                    dve.wait_ge(S["th"], n - 1)
                for q in range(2):
                    g = 2 * pr + q
                    last = V.scalar_tensor_tensor(
                        hw[n % 2][:, q, :], sg[n % 2][:, q, :],
                        xe[i % XS][:, g, DIM + GRP * g + i:DIM + GRP * g + i + 1],
                        bank[2 + n % 2][:, (2 * q + 1) * FF:(2 * q + 2) * FF], ALU.mult, ALU.mult)
                last.then_inc(S["h"], 1)

            def y_out(n):
                dve.wait_ge(S["dn"], n + 1)
                for s in range(NSUM):
                    if sums_after(2 * (n - YS + 1), s) > 0:
                        dve.wait_ge(s_sum[s], sums_after(2 * (n - YS + 1), s))
                V.tensor_copy(ysb[n % YS], bank[6 + n % 2][:, :].rearrange("p (q m) -> p q m", q=2)
                              ).then_inc(S["y_ok"], 1)
            def add_sums(k, q):
                s, ts = CLOSING[k], slice(q * TILES // OUTS, (q + 1) * TILES // OUTS)
                dve.wait_ge(s_acc[s][q], 16)
                if k:
                    dve.wait_ge(S["added"], (k - 1) * OUTS + q + 1)
                V.tensor_tensor(x[:, ts, :], x[:, ts, :], acc[s][:, ts, :], ALU.add).then_inc(S["added"], 1)

            NP = EXP // 2
            for n in range(1, NP + 3):
                if n < NP + 1:
                    hidden(n - 1)
                if n >= 3:
                    y_out(n - 3)
                q = n - (NP + 3 - OUTS)
                if q >= 0:
                    add_sums(0, q)
            for k in range(1, NSUM):
                for q in range(OUTS):
                    add_sums(k, q)

        @block.gpsimd
        def _(pool):
            G = nc.gpsimd
            pool.wait_ge(S["filled"], 16 * EPG)
            for t in range(TILES):
                pool.wait_ge(S["rows"], t + 1)
                pool.wait_ge(S["weights"], t + 1)
                for m in range(t * TOPK, (t + 1) * TOPK):
                    if m == TILES * TOPK - 5:
                        G.memset(mark_sb, 0.0).then_inc(S["near_spread"], 1)
                    G.indirect_dma_start(
                        out=xe_table[:, :], out_offset=bass.IndirectOffsetOnAxis(ap=rows8[:, m:m + 1], axis=0),
                        in_=hn[:, t, :], in_offset=None,
                        bounds_check=EXP * CAP - 1, oob_is_err=False).then_inc(S["spread"], 16)
            pool.wait_ge(S["zeroed"], 16 * NSUM)
            for n in range(EXP // 2):
                i, pr = n // 4, n % 4
                pool.wait_ge(S["y_ok"], n + 1)
                for q in range(2):
                    m = 2 * n + q
                    s = TABLE[m]
                    if sums_after(m, s):
                        pool.wait_ge(s_sum[s], sums_after(m, s))
                    G.indirect_dma_start(
                        out=sums[s][:, :],
                        out_offset=bass.IndirectOffsetOnAxis(
                            ap=xe[i % XS][:, 2 * pr + q, C_NUM:C_NUM + 1].bitcast(u32), axis=0),
                        in_=ysb[n % YS][:, q, :], in_offset=None, compute_op=ALU.add).then_inc(s_sum[s], 16)


def constants():
    import numpy as np
    c = np.zeros((P, C_ALL), np.float32)
    c[:, C_IDENT:C_IDENT + P] = np.eye(P)
    e = np.arange(EXP)
    c[:, C_KEY:C_KEY + EXP] = NOROW - ((e % EPG) * GRP * CAP + e // EPG) - GRP * PICKED
    c[:, C_TOK:C_TOK + TILES] = np.arange(P)[:, None] + P * np.arange(TILES)
    inv = (1.0 / np.float32(10000.0) ** (np.arange(0, DC, 2, dtype=np.float32) / np.float32(DC))).astype(np.float32)
    fr = np.arange(KEYS, dtype=np.float32)[:, None] * inv[None, :]
    cos, sin = np.repeat(np.cos(fr), 2, -1), np.repeat(np.sin(fr), 2, -1)
    sin[:, :DC // 2] *= -1.0
    c[:, C_COS:C_COS + DC] = np.tile(cos, (P // KEYS, 1))
    c[:, C_SIN:C_SIN + DC] = np.tile(sin, (P // KEYS, 1))
    c[:, C_TRI:C_TRI + P] = np.triu(np.ones((P, P)), 1) - PICKED * np.eye(P)
    return c


def empty_row():
    import numpy as np
    r = np.zeros((P, ROW), np.float32)
    r[:, C_NUM] = (TOK + np.arange(P)).astype(np.uint32).view(np.float32)
    return r


def kernel(**inputs):
    import numpy as np
    import concourse.bacc as bacc
    from concourse.bass_utils import run_bass_kernel_spmd

    v = {k.removeprefix("L0_"): np.asarray(a) for k, a in inputs.items()}

    def pack(w):
        e, r, c = w.shape
        return w.reshape(GRP, EPG, r // P, P, c).transpose(1, 3, 0, 2, 4)
    gate, up = pack(v["ffn_w_gate"]), pack(v["ffn_w_up"])
    d = {
        "x": v["x"].reshape(TOK, DIM),
        "ctx": v["ctx_512"].reshape(2, P, DC).transpose(1, 0, 2),
        "const": constants(),
        "empty": empty_row(),
        "wq": v["xattn_Wq"].reshape(HEADS, HK, DIM).transpose(1, 0, 2),
        "wkcq": v["xattn_w_kc_q"].reshape(HEADS, HK, QC, QP).transpose(3, 0, 2, 1),
        "wqr": v["xattn_W_qr"].reshape(HEADS, QC, QP, RK).transpose(2, 0, 1, 3),
        "wkr": v["xattn_W_kr"].reshape(PAIRS, 2, DC, RK).transpose(1, 3, 0, 2).reshape(2 * RK, PAIRS, DC),
        "wkv": v["xattn_w_kc_kv"].transpose(1, 0, 2),
        "wo": v["xattn_Wo"].reshape(DIM, HEADS, HK).transpose(2, 1, 0),
        "rw": v["ffn_router_weight"].reshape(EXP, CH, P).transpose(2, 1, 0),
        "ebias": np.tile(v["ffn_e_bias"].reshape(1, EXP), (P, 1)),
        "shw": np.concatenate([v[n].reshape(CH, P, FF).transpose(1, 0, 2) for n in ("ffn_sh_gate", "ffn_sh_up")], 1),
        "shd": v["ffn_sh_down"],
        "wgu": np.concatenate([gate, up], 4).reshape(EPG, P, GRP, CH, 2 * FF),
        "wdn": v["ffn_w_down"].reshape(GRP, EPG, FF, DIM).transpose(1, 2, 0, 3),
    }
    nc = bacc.Bacc("TRN2", target_bir_lowering=False, num_devices=1)
    arrays, aps = {}, {}
    for name, arr in d.items():
        arr = np.ascontiguousarray(arr)
        arrays[f"in_{name}"] = arr
        aps[name] = nc.dram_tensor(f"in_{name}", arr.shape, mybir.dt.float32, kind="ExternalInput").ap()
    out = nc.dram_tensor("out", (TOK, DIM), mybir.dt.float32, kind="ExternalOutput").ap()
    program(nc, aps, out)
    r = run_bass_kernel_spmd(nc, [arrays], core_ids=[0])
    return r.results[0]["out"].reshape(BATCH, SEQ, DIM)
```
